# Optimizing a Trainium2 kernel written in Bass

```python
import numpy as np
import jax
import jax.numpy as jnp

def _softmax(x, axis=-1):
    return jax.nn.softmax(x, axis=axis)

def _gelu(x):
    return jax.nn.gelu(x, approximate=True)

def _silu(x):
    return jax.nn.silu(x)

def _sigmoid(x):
    return jax.nn.sigmoid(x)

def _layernorm(x, axis=-1, eps=1e-05):
    m = jnp.mean(x, axis=axis, keepdims=True)
    v = jnp.var(x, axis=axis, keepdims=True)
    return (x - m) / jnp.sqrt(v + eps)

def _scatter_add(tgt, idx, src, axis=0):
    return tgt.at[idx].add(src)

def _segment_sum(src, seg, n):
    return jax.ops.segment_sum(src, seg, n)
kernel_name = 'mk_sandwich_d1_jaxref_r4_69f4ca'

def setup_inputs(seed: int=0):
    np.random.seed(seed)
    _w = jnp.asarray

    def _L0_attn_setup():
        import jax, jax.numpy as jnp
        import numpy as np
        D_MODEL = 256
        N_HEADS = 16
        N_GROUPS = 4
        D_HEAD = D_MODEL // N_HEADS
        HPG = N_HEADS // N_GROUPS
        B, T = (2, 512)

        def _rope(x):
            t, d = (x.shape[2], x.shape[3])
            pos = jnp.arange(t, dtype=jnp.float32)[:, None]
            freq = jnp.exp(-(jnp.arange(0, d, 2, dtype=jnp.float32) / d) * jnp.log(jnp.float32(10000.0)))
            angle = pos * freq
            cos, sin = (jnp.cos(angle), jnp.sin(angle))
            xe, xo = (x[..., ::2], x[..., 1::2])
            re = xe * cos - xo * sin
            ro = xe * sin + xo * cos
            return jnp.stack([re, ro], axis=-1).reshape(x.shape)
        key = jax.random.key(seed)
        ks = jax.random.split(key, 10)
        s = 0.02
        return {'x': jax.random.normal(ks[0], (B, T, D_MODEL), dtype=jnp.float32), 'Wq': jax.random.normal(ks[1], (D_MODEL, D_MODEL), dtype=jnp.float32) * s, 'bq': jax.random.normal(ks[2], (D_MODEL,), dtype=jnp.float32) * s, 'Wk': jax.random.normal(ks[3], (D_MODEL, N_GROUPS * D_HEAD), dtype=jnp.float32) * s, 'bk': jax.random.normal(ks[4], (N_GROUPS * D_HEAD,), dtype=jnp.float32) * s, 'Wv': jax.random.normal(ks[5], (D_MODEL, N_GROUPS * D_HEAD), dtype=jnp.float32) * s, 'bv': jax.random.normal(ks[6], (N_GROUPS * D_HEAD,), dtype=jnp.float32) * s, 'Wo': jax.random.normal(ks[7], (D_MODEL, D_MODEL), dtype=jnp.float32) * s, 'bo': jax.random.normal(ks[8], (D_MODEL,), dtype=jnp.float32) * s}
    _L0_attn_in = _L0_attn_setup()

    def _L0_ffn_setup():
        import jax, jax.numpy as jnp
        import numpy as np
        B, S, D = (2, 512, 256)
        I = 128
        E = 16
        TOP_K = 2

        def _mlp(x, wg, wu, wd):
            return jnp.einsum('bsi,id->bsd', jax.nn.silu(x @ wg) * (x @ wu), wd)
        key = jax.random.key(seed)
        ks = jax.random.split(key, 10)
        sc_d = 1.0 / np.sqrt(D)
        sc_i = 1.0 / np.sqrt(I)
        return {'x': jax.random.normal(ks[0], (B, S, D), dtype=jnp.float32), 'gate_w': jax.random.normal(ks[1], (D, E), dtype=jnp.float32) * sc_d, 'gate_b': jnp.zeros((E,), dtype=jnp.float32), 'shared_wg': jax.random.normal(ks[2], (D, I), dtype=jnp.float32) * sc_d, 'shared_wu': jax.random.normal(ks[3], (D, I), dtype=jnp.float32) * sc_d, 'shared_wd': jax.random.normal(ks[4], (I, D), dtype=jnp.float32) * sc_i, 'experts_wg': jax.random.normal(ks[5], (E, D, I), dtype=jnp.float32) * sc_d, 'experts_wu': jax.random.normal(ks[6], (E, D, I), dtype=jnp.float32) * sc_d, 'experts_wd': jax.random.normal(ks[7], (E, I, D), dtype=jnp.float32) * sc_i}
    _L0_ffn_in = _L0_ffn_setup()
    _d = {'L0_attn_x': _L0_attn_in['x'], 'L0_attn_Wq': _L0_attn_in['Wq'], 'L0_attn_bq': _L0_attn_in['bq'], 'L0_attn_Wk': _L0_attn_in['Wk'], 'L0_attn_bk': _L0_attn_in['bk'], 'L0_attn_Wv': _L0_attn_in['Wv'], 'L0_attn_bv': _L0_attn_in['bv'], 'L0_attn_Wo': _L0_attn_in['Wo'], 'L0_attn_bo': _L0_attn_in['bo'], 'L0_ffn_gate_w': _L0_ffn_in['gate_w'], 'L0_ffn_gate_b': _L0_ffn_in['gate_b'], 'L0_ffn_shared_wg': _L0_ffn_in['shared_wg'], 'L0_ffn_shared_wu': _L0_ffn_in['shared_wu'], 'L0_ffn_shared_wd': _L0_ffn_in['shared_wd'], 'L0_ffn_experts_wg': _L0_ffn_in['experts_wg'], 'L0_ffn_experts_wu': _L0_ffn_in['experts_wu'], 'L0_ffn_experts_wd': _L0_ffn_in['experts_wd']}
    _x0 = _d['L0_attn_x']
    _d['L0_attn_x'] = jax.random.normal(jax.random.fold_in(jax.random.key(seed), 1), (32, 512, 256), dtype=_x0.dtype)
    del _x0
    return _d

def reference(L0_attn_x, L0_attn_Wq, L0_attn_bq, L0_attn_Wk, L0_attn_bk, L0_attn_Wv, L0_attn_bv, L0_attn_Wo, L0_attn_bo, L0_ffn_gate_w, L0_ffn_gate_b, L0_ffn_shared_wg, L0_ffn_shared_wu, L0_ffn_shared_wd, L0_ffn_experts_wg, L0_ffn_experts_wu, L0_ffn_experts_wd):

    def _L0_attn_ref(x, Wq, bq, Wk, bk, Wv, bv, Wo, bo):
        import jax, jax.numpy as jnp
        import numpy as np
        D_MODEL = 256
        N_HEADS = 16
        N_GROUPS = 4
        D_HEAD = D_MODEL // N_HEADS
        HPG = N_HEADS // N_GROUPS
        B, T = (2, 512)

        def _rope(x):
            t, d = (x.shape[2], x.shape[3])
            pos = jnp.arange(t, dtype=jnp.float32)[:, None]
            freq = jnp.exp(-(jnp.arange(0, d, 2, dtype=jnp.float32) / d) * jnp.log(jnp.float32(10000.0)))
            angle = pos * freq
            cos, sin = (jnp.cos(angle), jnp.sin(angle))
            xe, xo = (x[..., ::2], x[..., 1::2])
            re = xe * cos - xo * sin
            ro = xe * sin + xo * cos
            return jnp.stack([re, ro], axis=-1).reshape(x.shape)
        b, t, _ = x.shape
        q = (x @ Wq + bq).reshape(b, t, N_HEADS, D_HEAD).transpose(0, 2, 1, 3)
        k = (x @ Wk + bk).reshape(b, t, N_GROUPS, D_HEAD).transpose(0, 2, 1, 3)
        v = (x @ Wv + bv).reshape(b, t, N_GROUPS, D_HEAD).transpose(0, 2, 1, 3)
        k = jnp.repeat(k, HPG, axis=1)
        v = jnp.repeat(v, HPG, axis=1)
        q = _rope(q)
        k = _rope(k)
        scale = jnp.float32(np.sqrt(D_HEAD))
        scores = jnp.einsum('bhtd,bhsd->bhts', q, k) / scale
        causal = jnp.tril(jnp.ones((t, t), dtype=bool))
        scores = jnp.where(causal, scores, -jnp.inf)
        probs = jax.nn.softmax(scores, axis=-1)
        attn = jnp.einsum('bhts,bhsd->bhtd', probs, v)
        out = attn.transpose(0, 2, 1, 3).reshape(b, t, N_HEADS * D_HEAD)
        return out @ Wo + bo

    def _L0_ffn_ref(x, gate_w, gate_b, shared_wg, shared_wu, shared_wd, experts_wg, experts_wu, experts_wd):
        import jax, jax.numpy as jnp
        import numpy as np
        B, S, D = (2, 512, 256)
        I = 128
        E = 16
        TOP_K = 2

        def _mlp(x, wg, wu, wd):
            return jnp.einsum('bsi,id->bsd', jax.nn.silu(x @ wg) * (x @ wu), wd)
        router_logits = jax.nn.sigmoid(x @ gate_w + gate_b)
        expert_values, expert_indices = jax.lax.top_k(router_logits, k=TOP_K)
        expert_values = expert_values / jnp.sum(expert_values, axis=-1, keepdims=True)
        hg = jnp.einsum('bsd,edi->bsei', x, experts_wg)
        hu = jnp.einsum('bsd,edi->bsei', x, experts_wu)
        all_outputs = jnp.einsum('bsei,eid->bsed', jax.nn.silu(hg) * hu, experts_wd)
        selected = jnp.take_along_axis(all_outputs, expert_indices[..., None], axis=2)
        expert_weighted = jnp.sum(expert_values[..., None] * selected, axis=2)
        return x + _mlp(x, shared_wg, shared_wu, shared_wd) + expert_weighted
    x = L0_attn_x
    x = x + _layernorm(_L0_attn_ref(_layernorm(x, axis=-1), L0_attn_Wq, L0_attn_bq, L0_attn_Wk, L0_attn_bk, L0_attn_Wv, L0_attn_bv, L0_attn_Wo, L0_attn_bo), axis=-1)
    x = x + _layernorm(_L0_ffn_ref(_layernorm(x, axis=-1), L0_ffn_gate_w, L0_ffn_gate_b, L0_ffn_shared_wg, L0_ffn_shared_wu, L0_ffn_shared_wd, L0_ffn_experts_wg, L0_ffn_experts_wu, L0_ffn_experts_wd), axis=-1)
    return x

_drawn_inputs = setup_inputs


def setup_inputs(seed=0):
    import zlib

    import numpy as np

    out = dict(_drawn_inputs(seed))
    spreads = {'L0_ffn_gate_b': (0.0, 0.1)}
    factors = {'L0_attn_bq': 7.943, 'L0_attn_bk': 26.738}
    for name, (base, spread) in spreads.items():
        noise = np.random.default_rng([zlib.crc32(name.encode()), seed]).standard_normal(out[name].shape)
        drawn = base * np.exp(spread * noise) if base else spread * noise
        out[name] = jnp.asarray(drawn.astype(out[name].dtype))
    for name, factor in factors.items():
        out[name] = (out[name] * factor).astype(out[name].dtype)
    return out
```

```python
from contextlib import ExitStack

import numpy as np

import concourse.bass as bass
from concourse import mybir

F32 = mybir.dt.float32
BF16 = mybir.dt.bfloat16
I32 = mybir.dt.int32
U32 = mybir.dt.uint32
ALU = mybir.AluOpType
ACT = mybir.ActivationFunctionType
AX_X = mybir.AxisListType.X

P = 128
B, T, D = 32, 512, 256
NT = T // P
NC = D // P
H, G, DH = 16, 4, 16
HG = H // G
E, I = 16, 128
TOKENS = B * T
PARTS = 3
BLOCKS = [(0, 0), (1, 0), (2, 0), (0, 1), (1, 1), (0, 2)]
KR = len(BLOCKS) * DH
KM = KR + PARTS
MASKED = -3.0e38
EPS = 1e-5
TILES = TOKENS * 2 // P + E
LIST = (E - 1) * TOKENS + TILES * P
RSQRT_SEED = float(0x5F3759DF)

MAX_UNITS = [(0, 0, 4, 128, 128), (1, 0, 4, 256, 256), (2, 0, 2, 384, 512), (2, 2, 2, 384, 512),
             (3, 0, 2, 512, 512), (3, 2, 2, 512, 512)]
EXP_UNITS = [(0, 0, 2, 512, 512), (0, 2, 2, 512, 512), (1, 0, 2, 384, 512), (1, 2, 2, 384, 512),
             (2, 0, 4, 256, 256), (3, 0, 4, 128, 128)]
NU = 6
UB = G * NU
MAX_LEAD = 9

MISC = [(0, "xt", 0), (1, "xt", 1), (2, "ot", 0), (2, "qa", 0), (3, "ot", 1), (3, "qb", 0), (3, "mt", 1),
        (4, "ot", 2), (4, "qa", 1), (5, "ot", 3), (5, "qb", 1), (6, "qa", 2), (7, "qb", 2), (8, "v", 0),
        (9, "at", 0), (9, "mt", 2), (10, "at", 1), (11, "op", 0), (12, "op", 1), (15, "mt", 3),
        (18, "ht", 0), (19, "ht", 1), (20, "rt", 0), (21, "mt", 4), (23, "cn", 0)]
OF_NEXT = ("xt", "qa", "qb", "v")
OF_LAST = ("ot", "at", "op", "ht", "rt", "cn")


class Batch:

    def __init__(self, offset, pair=None):
        self.offset, self.pair = offset, pair
        self.n = offset if pair is None else 2 * pair + offset
        self.parity = offset % 2
        self.half = offset // 2 if pair is None else pair + offset // 2

    def plus(self, k):
        return Batch(self.offset + k, self.pair)

    @property
    def exists(self):
        return self.pair is not None or 0 <= self.offset < B

    def later_than(self, k):
        return self.pair is not None or self.offset >= k


def active(cur, step, arg):
    if step in OF_NEXT:
        return cur.plus(1).exists
    if step in OF_LAST:
        return cur.plus(-1).exists
    return cur.plus(arg // G).exists


def fills(cur):
    return sum(active(cur, s, a) for _, s, a in MISC)


def misc_number(cur, pos):
    before = sum(active(cur, s, a) for _, s, a in MISC[:pos])
    if cur.pair is None:
        return sum(fills(Batch(k)) for k in range(-1, cur.offset)) + before
    return sum(fills(Batch(k)) for k in (-1, 0)) + len(MISC) * (cur.n - 1) + before


def position(step, arg):
    return [m[1:] for m in MISC].index((step, arg))


def rounds(eng, body):
    for k in (-1, 0):
        body(Batch(k))
    with eng.Fori(0, (B - 4) // 2) as pair:
        for u in (1, 2):
            body(Batch(u, pair))
    for k in range(B - 3, B + 1):
        body(Batch(k))


class Pause:

    def __init__(self, eng, cell, zeros=None, done=None):
        self.eng, self.cell, self.zeros, self.done = eng, cell[:, 0:1], zeros, done

    def __call__(self, number=None, later=False):
        if self.done is None:
            self.eng.memset(self.cell, 0.0)
            return
        if later:
            self.eng.wait_ge(self.done, number)
        self.eng.tensor_tensor(self.cell, self.zeros, self.zeros, ALU.add).then_inc(self.done, 1)


def wait_all(eng, *waits):
    values = [v if isinstance(v, int) else eng.snap(v) for _, v in waits]
    for (sem, _), v in zip(waits, values):
        eng.wait_ge(sem, v)


class Steps:

    def __init__(self, eng, sem, per):
        self.eng, self.sem, self.per = eng, sem, per

    def begin(self, n):
        self.base, self.c = self.per * n, 0

    def did(self, ins):
        ins.then_inc(self.sem, 1)
        self.c += 1

    def settle(self):
        self.eng.wait_ge(self.sem, self.base + self.c)

    def end(self):
        assert self.c == self.per, (self.c, self.per)


RSQRT_STEPS = 13


def rsqrt(dve, steps, out, var, work):
    steps.did(dve.tensor_scalar(work[0], var, EPS, None, ALU.add))
    steps.settle()
    steps.did(dve.tensor_scalar(out.bitcast(I32), work[0].bitcast(I32), 1, None, ALU.arith_shift_right))
    steps.did(dve.tensor_scalar(work[1], work[0], -0.5, None, ALU.mult))
    steps.settle()
    steps.did(dve.tensor_scalar(out.bitcast(I32), out.bitcast(I32), -1.0, RSQRT_SEED, ALU.mult, ALU.add))
    steps.settle()
    for _ in range(3):
        steps.did(dve.tensor_tensor(work[0], out, out, ALU.mult))
        steps.settle()
        steps.did(dve.tensor_tensor(work[0], work[0], work[1], ALU.mult))
        steps.settle()
        steps.did(dve.scalar_tensor_tensor(out=out, in0=work[0], scalar=1.5, in1=out, op0=ALU.add, op1=ALU.mult))
        steps.settle()


def layer(nc, a, out):
    ctx = ExitStack()
    with ctx:
        def sb(name, shape, dt=F32):
            return ctx.enter_context(nc.sbuf_tensor(name, shape, dt))

        def sem(name):
            return ctx.enter_context(nc.semaphore(name))

        def dram(name, shape, dt=F32):
            return nc.dram_tensor(name, shape, dt, kind="Internal").ap()

        q_parts_dram = dram("q_parts_dram", [2, H, PARTS, DH, T], BF16)
        k_parts_dram = dram("k_parts_dram", [2, G, PARTS, DH, T], BF16)
        x1_dram = dram("x1_dram", [B, T, D])
        h2_dram = dram("h2_dram", [B, T, D])
        id_list = dram("id_list", [LIST, 1], I32)
        y_dram = dram("y_dram", [TILES * P, D])

        wq = sb("wq", [P, 2, NC, D])
        wk = sb("wk", [P, 2, NC, G * DH])
        bq = sb("bq", [P, 2, NC])
        bk = sb("bk", [G * DH, 2])
        rope = sb("rope", [P, 2, 2, T])
        wv = sb("wv", [P, NC, G * 2 * DH])
        bv = sb("bv", [P, G * 2 * DH])
        wo = sb("wo", [P, NC, D])
        bo = sb("bo", [P, D])
        gate_w = sb("gate_w", [P, NC, E])
        gate_b = sb("gate_b", [P, E])
        wgu = sb("wgu", [P, E + 1, NC, 2 * I])
        wd = sb("wd", [P, E + 1, D])
        ident = sb("ident", [P, P])
        ident_bf = sb("ident_bf", [P, P], BF16)
        mask_max = sb("mask_max", [P, P], BF16)
        mask_exp = sb("mask_exp", [P, P], BF16)
        before = sb("before", [P, P], BF16)
        ones_bf = sb("ones_bf", [P, P], BF16)
        iota_e = sb("iota_e", [P, E])
        token = sb("token", [P, NT])
        zeros = sb("zeros", [P, 544], I32)
        routed_e = sb("routed_e", [P, B, NT, 2])
        routed_pos = sb("routed_pos", [P, B, NT, 2])
        routed_w = sb("routed_w", [P, B, NT, 2])
        counts = sb("counts", [P, NT + 1, E])

        pool_cell, dve_cell = sb("pool_cell", [1, 2]), sb("dve_cell", [1, 2])
        zero_col = sb("zero_col", [P, 1])

        weights_in = sem("weights_in")
        consts = sem("consts")
        zeroed = sem("zeroed")
        experts_in = sem("experts_in")
        x1_stored, h2_stored = sem("x1_stored"), sem("h2_stored")
        scattered = [sem(f"scattered{k}") for k in range(2)]

        attention_phase(nc, a, locals())
        expert_phases(nc, a, out, locals())


def attention_phase(nc, a, v):
    (q_parts_dram, k_parts_dram, x1_dram, h2_dram, id_list) = (
        v[n] for n in ("q_parts_dram", "k_parts_dram", "x1_dram", "h2_dram", "id_list"))
    (wq, wk, bq, bk, rope, wv, bv, wo, bo, gate_w, gate_b, wgu, wd) = (
        v[n] for n in ("wq", "wk", "bq", "bk", "rope", "wv", "bv", "wo", "bo", "gate_w", "gate_b", "wgu", "wd"))
    (ident, ident_bf, mask_max, mask_exp, before, ones_bf, iota_e, token, zeros) = (
        v[n] for n in ("ident", "ident_bf", "mask_max", "mask_exp", "before", "ones_bf", "iota_e", "token",
                       "zeros"))
    (routed_e, routed_pos, routed_w, counts, pool_cell, dve_cell, zero_col) = (
        v[n] for n in ("routed_e", "routed_pos", "routed_w", "counts", "pool_cell", "dve_cell", "zero_col"))
    (weights_in, experts_in, consts, zeroed, x1_stored, h2_stored, scattered) = (
        v[n] for n in ("weights_in", "experts_in", "consts", "zeroed", "x1_stored", "h2_stored", "scattered"))

    ctx = ExitStack()
    with ctx:
        def sb(name, shape, dt=F32):
            return ctx.enter_context(nc.sbuf_tensor(name, shape, dt))

        def psum(name, shape):
            return ctx.enter_context(nc.psum_tensor(name, shape, F32))

        def sem(name):
            return ctx.enter_context(nc.semaphore(name))

        x_in = sb("x_in", [P, 2, NT, D])
        h1 = sb("h1", [P, NT, D])
        h1t = sb("h1t", [P, NC, T])
        roped = sb("roped", [P, 2, T])
        rest = sb("rest", [P, T])
        q_parts = sb("q_parts", [P, NC, PARTS, T], BF16)
        k_parts = sb("k_parts", [G * DH, PARTS, T], BF16)
        qs = sb("qs", [P, 2, H, T], BF16)
        ks = sb("ks", [P, 2, G, T], BF16)
        va = sb("va", [P, 2, NT, G * 2 * DH])
        negmax = sb("negmax", [P, 2, NT, HG])
        negmax_rest = sb("negmax_rest", [P, NT, HG])
        negmax_parts = sb("negmax_parts", [P, 2, NT, PARTS, HG], BF16)
        negmax_t = sb("negmax_t", [PARTS * HG, T], BF16)
        probs = sb("probs", [P, 2, 2 * T])
        heads_t = sb("heads_t", [P, G, T])
        denom = sb("denom", [P, H])
        heads = sb("heads", [P, NT, D])
        headst = sb("headst", [P, NC, T])
        proj = sb("proj", [P, NT, D])
        x_res = sb("x_res", [P, NT, D])
        x1 = sb("x1", [P, NT, D])
        h2 = sb("h2", [P, NT, D])
        h2t = sb("h2t", [P, NC, T])
        stats = sb("stats", [P, NT, 6])
        moments = sb("moments", [P, NT, 2])
        rstd = sb("rstd", [P, NT])
        work = [sb(f"work{k}", [P, NT]) for k in range(2)]
        logits = sb("logits", [P, NT, E])
        gates = sb("gates", [P, NT, E])
        top = sb("top", [P, NT, 8])
        top_at = sb("top_at", [P, NT, 8], U32)
        expert = sb("expert", [P, NT, 2])
        top_sum = sb("top_sum", [P, NT])
        onehot = sb("onehot", [P, NT, 2, E])
        chosen = sb("chosen", [P, NT, E], BF16)
        place = sb("place", [P, NT, E])
        placed = sb("placed", [P, NT, 2, E])
        slot = [sb(f"slot{k}", [P, NT, 2], U32) for k in range(2)]
        token_i = [sb(f"token_i{k}", [P, NT], I32) for k in range(2)]

        ps_exp = psum("ps_exp", [P, 2, 2 * T])
        ps_max = psum("ps_max", [P, 2 * T])
        ps_out = psum("ps_out", [P, T])
        ps_misc = psum("ps_misc", [P, T])

        x_loaded = [sem(f"x_loaded{k}") for k in range(2)]
        x_res_loaded = sem("x_res_loaded")
        stack_ones = sem("stack_ones")
        paused = sem("paused")
        ln1_steps = sem("ln1_steps")
        h1_ready = sem("h1_ready")
        misc_full, misc_taken = sem("misc_full"), sem("misc_taken")
        split_steps = sem("split_steps")
        parts_stored = [sem(f"parts_stored{k}") for k in range(2)]
        stacks_loaded = [sem(f"stacks_loaded{k}") for k in range(2)]
        max_scored, max_reduced = sem("max_scored"), sem("max_reduced")
        negmax_steps = sem("negmax_steps")
        negmax_loaded = [sem(f"negmax_loaded{k}") for k in range(2)]
        scored, exped, weighed = sem("scored"), sem("exped"), sem("weighed")
        heads_t_ready = sem("heads_t_ready")
        post_steps = sem("post_steps")
        x1_ready, h2_ready = sem("x1_ready"), sem("h2_ready")
        gates_exped = sem("gates_exped")
        chosen_ready = sem("chosen_ready")
        slots_ready = sem("slots_ready")

        n_weights = 0
        SPLITS = 5
        PER_STORE = 16 * 3 * PARTS
        Q_LOADS = [(0, 3, 0), (3 * DH, 2, 0), (5 * DH, 1, 0)]
        PER_LOAD = 16 * (len(Q_LOADS) + len(BLOCKS))

        def wait_misc(eng, cur, step, arg):
            eng.wait_ge(misc_full, misc_number(cur, position(step, arg)) + 1)

        def max_unit(cur, n):
            m = n + MAX_LEAD
            b = cur.plus(m // UB)
            return b, (m % UB) // NU, m % NU

        block = ctx.enter_context(nc.Block())

        @block.sync
        def _(sp):
            loads = [(wq[:, k], a[f"wq{k}"].rearrange("(c p) n -> p c n", p=P)) for k in range(2)]
            loads += [(wk[:, k], a[f"wk{k}"].rearrange("(c p) n -> p c n", p=P)) for k in range(2)]
            loads += [(bq[:, :, :], a["bq"]), (bk[:, :], a["bk"]), (rope[:, :, :, :], a["rope"]),
                      (wv[:, :, :], a["wv"].rearrange("(c p) n -> p c n", p=P)),
                      (bv[:, :], a["bv"].partition_broadcast(P)), (bo[:, :], a["bo"].partition_broadcast(P)),
                      (wo[:, :, :], a["wo"].rearrange("(c p) n -> p c n", p=P)),
                      (gate_w[:, :, :], a["gate_w"].rearrange("(c p) n -> p c n", p=P)),
                      (gate_b[:, :], a["gate_b"].partition_broadcast(P))]
            sp.dma_start(x_in[:, 0], a["x"][0].rearrange("(j p) d -> p j d", p=P)).then_inc(x_loaded[0], 16)
            for dst, src in loads:
                sp.dma_start(dst, src).then_inc(weights_in, 16)
            assert len(loads) == N_LOADS
            sp.wait_ge(consts, N_CONSTS)
            rows = LIST // 544
            done = 0
            while done < rows:
                k = min(P, rows - done)
                sp.dma_start(id_list[done * 544:(done + k) * 544].rearrange("(p n) o -> p (n o)", p=k),
                             zeros[0:k, :]).then_inc(zeroed, 16)
                done += k
            sp.dma_start(id_list[rows * 544:LIST].rearrange("n o -> o n"), zeros[0:1, 0:LIST - rows * 544]) \
                .then_inc(zeroed, 16)
            for e in range(E):
                sp.dma_start(wgu[:, e, :, 0:I], a["eg"][e].rearrange("(c p) n -> p c n", p=P)).then_inc(experts_in, 16)
                sp.dma_start(wgu[:, e, :, I:], a["eu"][e].rearrange("(c p) n -> p c n", p=P)).then_inc(experts_in, 16)
                sp.dma_start(wd[:, e, :], a["ed"][e]).then_inc(experts_in, 16)
            sp.dma_start(wgu[:, E, :, 0:I], a["sg"].rearrange("(c p) n -> p c n", p=P)).then_inc(experts_in, 16)
            sp.dma_start(wgu[:, E, :, I:], a["su"].rearrange("(c p) n -> p c n", p=P)).then_inc(experts_in, 16)
            sp.dma_start(wd[:, E, :], a["sd"]).then_inc(experts_in, 16)

            def store_parts(nxt, unit):
                waits = [(split_steps, 3 * SPLITS * nxt.n + SPLITS * (unit + 1))]
                if unit == 0 and nxt.later_than(2):
                    waits.append((stacks_loaded[nxt.parity], PER_LOAD * nxt.half))
                wait_all(sp, *waits)
                for part in range(PARTS):
                    if unit < NC:
                        hs = slice(unit * H // NC, (unit + 1) * H // NC)
                        sp.dma_start(q_parts_dram[nxt.parity, hs, part], q_parts[:, unit, part, :]) \
                            .then_inc(parts_stored[nxt.parity], 16)
                    else:
                        sp.dma_start(k_parts_dram[nxt.parity, :, part], k_parts[:, part, :]) \
                            .then_inc(parts_stored[nxt.parity], 16)

            def load_stacks(nxt):
                sp.wait_ge(parts_stored[nxt.parity], PER_STORE * (nxt.half + 1))
                src = q_parts_dram[nxt.parity]
                for row, n, first in Q_LOADS:
                    sp.dma_start(qs[row:row + n * DH, nxt.parity],
                                 src[:, first:first + n].rearrange("h a d t -> (a d) h t")) \
                        .then_inc(stacks_loaded[nxt.parity], 16)
                for k, (_, part) in enumerate(BLOCKS):
                    sp.dma_start(ks[k * DH:(k + 1) * DH, nxt.parity],
                                 k_parts_dram[nxt.parity, :, part].rearrange("g d t -> d g t")) \
                        .then_inc(stacks_loaded[nxt.parity], 16)

            def load_negmax(cur, pos, b, g):
                sp.wait_ge(misc_taken, misc_number(cur, pos) + 1)
                for part in range(PARTS):
                    sp.dma_start(qs[KR + part:KR + part + 1, b.parity, g * HG:(g + 1) * HG, :],
                                 negmax_t[part * HG:(part + 1) * HG, :]).then_inc(negmax_loaded[g % 2], 16)

            def body(cur):
                nxt, last = cur.plus(1), cur.plus(-1)
                for n in range(UB):
                    if n == 0 and nxt.plus(1).exists:
                        after = nxt.plus(1)
                        if after.later_than(2):
                            sp.wait_ge(h1_ready, after.n - 1)
                        sp.dma_start(x_in[:, after.parity], a["x"][after.n].rearrange("(j p) d -> p j d", p=P)) \
                            .then_inc(x_loaded[after.parity], 16)
                    if n == 1 and nxt.exists and nxt.later_than(2):
                        sp.wait_ge(scored, UB * (nxt.n - 1))
                    if n == 1 and last.exists:
                        if last.later_than(1):
                            sp.wait_ge(x1_ready, last.n)
                        sp.dma_start(x_res[:, :, :], a["x"][last.n].rearrange("(j p) d -> p j d", p=P)) \
                            .then_inc(x_res_loaded, 16)
                    if nxt.exists and n in (6, 8, 10):
                        store_parts(nxt, (n - 6) // 2)
                    if nxt.exists and n == 12:
                        load_stacks(nxt)
                    if n == 17 and last.exists:
                        sp.wait_ge(x1_ready, last.n + 1)
                        sp.dma_start(x1_dram[last.n].rearrange("(j p) d -> p j d", p=P), x1[:, :, :]) \
                            .then_inc(x1_stored, 16)
                    if n == 19 and last.exists:
                        sp.wait_ge(h2_ready, last.n + 1)
                        sp.dma_start(h2_dram[last.n].rearrange("(j p) d -> p j d", p=P), h2[:, :, :]) \
                            .then_inc(h2_stored, 16)
                    for pos, (at, step, g) in enumerate(MISC):
                        if at == n and step == "mt" and active(cur, step, g):
                            load_negmax(cur, pos, cur.plus(g // G), g % G)

            rounds(sp, body)

        @block.gpsimd
        def _(pool):
            pause = Pause(pool, pool_cell, zero_col[0:1, 0:1], paused)

            pool.memset(ident[:, :], 0.0).then_inc(consts, 1)
            pool.memset(ident_bf[:, :], 0.0).then_inc(consts, 1)
            pool.memset(mask_max[:, :], 0.0).then_inc(consts, 1)
            pool.memset(mask_exp[:, :], 0.0).then_inc(consts, 1)
            pool.memset(before[:, :], 0.0).then_inc(consts, 1)
            pool.memset(ones_bf[:, :], 1.0).then_inc(consts, 1)
            pool.memset(zeros[:, :], 0).then_inc(consts, 1)
            pool.memset(zero_col[:, :], 0.0).then_inc(consts, 1)
            pool.memset(counts[:, NT, :], 0.0).then_inc(consts, 1)
            pool.wait_ge(consts, 9)
            for m in (ident, ident_bf):
                pool.affine_select(out=m[:, :], in_=m[:, :], compare_op=ALU.not_equal, fill=1.0, base=0,
                                   pattern=[[-1, P]], channel_multiplier=1).then_inc(consts, 1)
            pool.affine_select(out=mask_max[:, :], in_=mask_max[:, :], compare_op=ALU.is_ge, fill=MASKED,
                               base=0, pattern=[[-1, P]], channel_multiplier=1).then_inc(consts, 1)
            pool.affine_select(out=mask_exp[:, :], in_=mask_exp[:, :], compare_op=ALU.is_ge, fill=MASKED,
                               base=0, pattern=[[1, P]], channel_multiplier=-1).then_inc(consts, 1)
            pool.affine_select(out=before[:, :], in_=before[:, :], compare_op=ALU.is_ge, fill=1.0,
                               base=0, pattern=[[-1, P]], channel_multiplier=1).then_inc(consts, 1)
            pool.iota(iota_e[:, :], pattern=[[1, E]], base=0, channel_multiplier=0,
                      allow_small_or_imprecise_dtypes=True).then_inc(consts, 1)
            pool.iota(token[:, :], pattern=[[P, NT]], base=0, channel_multiplier=1,
                      allow_small_or_imprecise_dtypes=True).then_inc(consts, 1)

            def split(cur, unit):
                nxt = cur.plus(1)
                n = G * DH if unit == NC else P
                parts = [k_parts[:, k, :] if unit == NC else q_parts[:, unit, k, :] for k in range(PARTS)]
                pool.wait_ge(misc_taken, misc_number(cur, position("qb", unit)) + 1)
                steps = Steps(pool, split_steps, 3 * SPLITS)
                steps.begin(nxt.n)
                steps.c = SPLITS * unit
                r = rest[0:n, :]
                if unit or nxt.later_than(1):
                    steps.settle()
                steps.did(pool.tensor_tensor(r, roped[0:n, 0, :], roped[0:n, 1, :], ALU.add))
                if unit == 0 and nxt.later_than(1):
                    b = nxt.plus(-1)
                    pool.wait_ge(parts_stored[b.parity], PER_STORE * (b.half + 1))
                for k in range(PARTS):
                    if k == PARTS - 1:
                        break
                    steps.settle()
                    steps.did(pool.tensor_tensor(parts[k], r, zero_col[0:n, :].to_broadcast([n, T]), ALU.add))
                    steps.settle()
                    steps.did(pool.tensor_tensor(parts[2] if k == 1 else r, r, parts[k], ALU.subtract))

            def scatter(last):
                pool.wait_ge(slots_ready, last.n + 1)
                pause(last.n, last.later_than(1))
                for j in range(NT):
                    for k in range(2):
                        pool.indirect_dma_start(
                            out=id_list[:, :], in_=token_i[last.parity][:, j:j + 1], in_offset=None,
                            out_offset=bass.IndirectOffsetOnAxis(ap=slot[last.parity][:, j, k:k + 1], axis=0),
                        ).then_inc(scattered[last.parity], 16)

            def body(cur):
                if cur.plus(1).exists:
                    for unit in range(NC + 1):
                        split(cur, unit)
                if cur.plus(-1).exists:
                    scatter(cur.plus(-1))
                if cur.pair is None and cur.offset == 0:
                    pool.wait_ge(zeroed, 16 * N_ZEROS)

            rounds(pool, body)

        @block.tensor
        def _(pe):
            pe.wait_ge(weights_in, 16 * N_LOADS)
            pe.wait_ge(stack_ones, 1)
            pe.wait_ge(consts, N_CONSTS)

            def misc(cur, pos):
                _, step, arg = MISC[pos]
                nxt, last = cur.plus(1), cur.plus(-1)
                number = misc_number(cur, pos)
                if cur.offset > -1 or pos > 0:
                    pe.wait_ge(misc_taken, number)
                if step == "xt":
                    pe.wait_ge(h1_ready, nxt.n + 1)
                    for j in range(NT):
                        ins = pe.transpose(ps_misc[:, j * P:(j + 1) * P], h1[:, j, arg * P:(arg + 1) * P],
                                           ident[:, :])
                elif step in ("qa", "qb"):
                    k = step == "qb"
                    for c in range(NC):
                        if arg < NC:
                            ins = pe.matmul(ps_misc[:, :], wq[:, k, c, arg * P:(arg + 1) * P], h1t[:, c, :],
                                            start=(c == 0), stop=(c == NC - 1))
                        else:
                            ins = pe.matmul(ps_misc[0:G * DH, :], wk[:, k, c, :], h1t[:, c, :],
                                            start=(c == 0), stop=(c == NC - 1))
                elif step == "v":
                    for j in range(NT):
                        for c in range(NC):
                            ins = pe.matmul(ps_misc[:, j * P:(j + 1) * P], h1t[:, c, j * P:(j + 1) * P],
                                            wv[:, c, :], start=(c == 0), stop=(c == NC - 1))
                elif step == "mt":
                    b, g = cur.plus(arg // G), arg % G
                    pe.wait_ge(negmax_steps, 4 * (G * b.n + g + 1))
                    for j in range(NT):
                        ins = pe.transpose(ps_misc[:, :].bitcast(BF16)[0:PARTS * HG, j * P:(j + 1) * P],
                                           negmax_parts[:, g % 2, j].rearrange("p a h -> p (a h)"), ident_bf[:, :])
                elif step == "ot":
                    pe.wait_ge(heads_t_ready, G * (last.n + 1))
                    for g in range(G):
                        ins = pe.transpose(ps_misc[:, g * P:(g + 1) * P], heads_t[:, g, arg * P:(arg + 1) * P],
                                           ident[:, :])
                elif step == "at":
                    for j in range(NT):
                        ins = pe.transpose(ps_misc[:, j * P:(j + 1) * P], heads[:, j, arg * P:(arg + 1) * P],
                                           ident[:, :])
                elif step == "op":
                    for k in range(2):
                        j = 2 * arg + k
                        for c in range(NC):
                            ins = pe.matmul(ps_misc[:, k * D:(k + 1) * D], headst[:, c, j * P:(j + 1) * P],
                                            wo[:, c, :], start=(c == 0), stop=(c == NC - 1))
                elif step == "ht":
                    pe.wait_ge(h2_ready, last.n + 1)
                    for j in range(NT):
                        ins = pe.transpose(ps_misc[:, j * P:(j + 1) * P], h2[:, j, arg * P:(arg + 1) * P],
                                           ident[:, :])
                elif step == "rt":
                    for j in range(NT):
                        for c in range(NC):
                            ins = pe.matmul(ps_misc[:, j * E:(j + 1) * E], h2t[:, c, j * P:(j + 1) * P],
                                            gate_w[:, c, :], start=(c == 0), stop=(c == NC - 1))
                elif step == "cn":
                    pe.wait_ge(chosen_ready, last.n + 1)
                    m = chosen[:, :, :].rearrange("p j e -> p (j e)")
                    pe.matmul(ps_misc[:, 0:NT * E], before[:, :], m, start=True, stop=True)
                    ins = pe.matmul(ps_misc[:, NT * E:2 * NT * E], ones_bf[:, :], m, start=True, stop=True)
                ins.then_inc(misc_full, 1)

            def score_max(cur, n):
                b, g, u = max_unit(cur, n)
                if not b.exists:
                    return
                j, h0, nh, width, stride = MAX_UNITS[u]
                if g == 0 and u == 0:
                    pe.wait_ge(stacks_loaded[b.parity], PER_LOAD * (b.half + 1))
                number = UB * b.n + NU * g + u
                if b.pair is not None or number > 0:
                    pe.wait_ge(max_reduced, number)
                for k in range(nh):
                    h = g * HG + h0 + k
                    at = k * stride
                    pe.matmul(ps_max[:, at:at + width], qs[0:KR, b.parity, h, j * P:(j + 1) * P],
                              ks[0:KR, b.parity, g, 0:width], start=True, stop=False)
                    ins = pe.matmul(ps_max[:, at + j * P:at + (j + 1) * P], ident_bf[:, :], mask_max[:, :],
                                    start=False, stop=True)
                ins.then_inc(max_scored, 1)

            def score_exp(b, n):
                g, u = n // NU, n % NU
                j, h0, nh, width, stride = EXP_UNITS[u]
                if u == 0:
                    pe.wait_ge(negmax_loaded[g % 2], 16 * PARTS * (2 * b.n + g // 2 + 1))
                if b.later_than(1) or n >= 2:
                    pe.wait_ge(exped, UB * b.n + n - 1)
                for k in range(nh):
                    at = k * stride
                    pe.matmul(ps_exp[:, n % 2, at:at + width], ks[0:KM, b.parity, g, j * P:(j + 1) * P],
                              qs[0:KM, b.parity, g * HG + h0 + k, j * P:T], start=True, stop=False)
                    ins = pe.matmul(ps_exp[:, n % 2, at:at + P], ident_bf[:, :], mask_exp[:, :],
                                    start=False, stop=True)
                ins.then_inc(scored, 1)

            def weigh(b, n):
                g, u = n // NU, n % NU
                j, h0, nh, width, stride = EXP_UNITS[u]
                pe.wait_ge(exped, UB * b.n + n + 1)
                if u == 0 and (b.later_than(1) or g > 0):
                    pe.wait_ge(heads_t_ready, G * b.n + g)
                for k in range(nh):
                    hh = h0 + k
                    ins = pe.matmul(ps_out[32 * hh:32 * hh + 32, j * P:T], va[:, b.parity, j, g * 32:(g + 1) * 32],
                                    probs[:, n % 2, k * stride:k * stride + width],
                                    start=(j == 0), stop=(j == NT - 1))
                ins.then_inc(weighed, 1)

            def body(cur):
                for n in range(UB):
                    if cur.exists:
                        score_exp(cur, n)
                    score_max(cur, n)
                    for pos, (at, step, arg) in enumerate(MISC):
                        if at == n and active(cur, step, arg):
                            misc(cur, pos)
                    if n > 0 and cur.exists:
                        weigh(cur, n - 1)
                    if n == 0 and cur.plus(-1).exists:
                        weigh(cur.plus(-1), UB - 1)

            rounds(pe, body)

        @block.scalar
        def _(act):
            def exp(b, n):
                j, h0, nh, width, stride = EXP_UNITS[n % NU]
                act.wait_ge(scored, UB * b.n + n + 1)
                if b.later_than(1) or n >= 2:
                    act.wait_ge(weighed, UB * b.n + n - 1)
                src = ps_exp[:, n % 2, 0:nh * stride].rearrange("p (h w) -> p h w", h=nh)[:, :, 0:width]
                dst = probs[:, n % 2, 0:nh * stride].rearrange("p (h w) -> p h w", h=nh)[:, :, 0:width]
                act.activation(dst, src, ACT.Exp).then_inc(exped, 1)

            def take(cur, pos):
                _, step, arg = MISC[pos]
                if step not in ("xt", "mt", "at", "ht"):
                    return
                nxt, last = cur.plus(1), cur.plus(-1)
                wait_misc(act, cur, step, arg)
                if step == "mt":
                    b, g = cur.plus(arg // G), arg % G
                    if b.pair is not None or b.offset > 0 or g > 0:
                        act.wait_ge(negmax_loaded[(g + 1) % 2],
                                    16 * PARTS * (2 * b.n + (g + 1) // 2))
                    act.copy(negmax_t[:, :], ps_misc[:, :].bitcast(BF16)[0:PARTS * HG, 0:T]) \
                        .then_inc(misc_taken, 1)
                else:
                    dst = {"xt": h1t, "at": headst, "ht": h2t}[step]
                    act.copy(dst[:, arg, :], ps_misc[:, :]).then_inc(misc_taken, 1)

            def body(cur):
                last = cur.plus(-1)
                for n in range(UB):
                    if cur.exists:
                        exp(cur, n)
                    for pos, (at, step, arg) in enumerate(MISC):
                        if at == n and active(cur, step, arg):
                            take(cur, pos)
                    if n == 20 and last.exists:
                        act.wait_ge(misc_taken, misc_number(cur, position("rt", 0)) + 1)
                        act.activation(gates[:, :, :], logits[:, :, :], ACT.Exp, scale=-1.0) \
                            .then_inc(gates_exped, 1)
                    if n % NU == 0:
                        b, g = (cur, n // NU - 1) if n else (last, G - 1)
                        if b.exists:
                            act.wait_ge(weighed, UB * b.n + NU * (g + 1))
                            if g == 0 and b.later_than(1):
                                act.wait_ge(misc_full, misc_number(b, position("ot", NT - 1)) + 1)
                            act.copy(heads_t[:, g, :], ps_out[:, :]).then_inc(heads_t_ready, 1)

            rounds(act, body)

        @block.vector
        def _(dve):
            pause = Pause(dve, dve_cell)

            dve.memset(ks[KR:P, :, :, :], 1.0).then_inc(stack_ones, 1)
            dve.wait_ge(weights_in, 16 * N_LOADS)
            dve.wait_ge(consts, N_CONSTS)
            ln = Steps(dve, ln1_steps, NT + NT + RSQRT_STEPS)
            post = Steps(dve, post_steps, POST_STEPS)

            def layernorm(steps, dst, src, last_sem):
                for j in range(NT):
                    steps.did(dve.bn_stats(stats[:, j, :], src[:, j, :]))
                steps.settle()
                pause()
                for j in range(NT):
                    steps.did(dve.bn_aggr(moments[:, j, :], stats[:, j, :]))
                steps.settle()
                rsqrt(dve, steps, rstd[:, :], moments[:, :, 1], [w[:, :] for w in work])
                for j in range(NT):
                    ins = dve.tensor_scalar(dst[:, j, :], src[:, j, :], moments[:, j, 0:1], rstd[:, j:j + 1],
                                            ALU.subtract, ALU.mult)
                    if last_sem is None:
                        steps.did(ins)
                if last_sem is not None:
                    ins.then_inc(last_sem, 1)

            def first_norm(nxt, cur):
                ln.begin(nxt.n)
                dve.wait_ge(x_loaded[nxt.parity], 16 * (nxt.half + 1))
                layernorm(ln, h1, x_in[:, nxt.parity], h1_ready)
                ln.end()

            def reduce_max(cur, n):
                b, g, u = max_unit(cur, n)
                if not b.exists:
                    return
                j, h0, nh, width, stride = MAX_UNITS[u]
                dve.wait_ge(max_scored, UB * b.n + NU * g + u + 1)
                src = ps_max[:, 0:nh * stride].rearrange("p (h w) -> p h w", h=nh)[:, :, 0:width]
                dve.tensor_reduce(negmax[:, g % 2, j, h0:h0 + nh], src, AX_X, ALU.max, negate=True) \
                    .then_inc(max_reduced, 1)
                if u == NU - 1:
                    dve.wait_ge(max_reduced, UB * b.n + NU * (g + 1))
                    parts = [negmax_parts[:, g % 2, :, k, :] for k in range(PARTS)]
                    steps = Steps(dve, negmax_steps, 4)
                    steps.begin(G * b.n + g)
                    steps.did(dve.tensor_copy(parts[0], negmax[:, g % 2]))
                    steps.settle()
                    steps.did(dve.tensor_tensor(negmax_rest[:, :, :], negmax[:, g % 2], parts[0], ALU.subtract))
                    steps.settle()
                    steps.did(dve.tensor_copy(parts[1], negmax_rest[:, :, :]))
                    steps.settle()
                    steps.did(dve.tensor_tensor(parts[2], negmax_rest[:, :, :], parts[1], ALU.subtract))

            def take(cur, pos):
                _, step, arg = MISC[pos]
                if step in ("xt", "mt", "at", "ht"):
                    return
                nxt, last = cur.plus(1), cur.plus(-1)
                wait_misc(dve, cur, step, arg)
                if step in ("qa", "qb"):
                    k = int(step == "qb")
                    if k == 0 and (nxt.later_than(1) or arg > 0):
                        if arg:
                            dve.wait_ge(split_steps, 3 * SPLITS * nxt.n + SPLITS * (arg - 1) + 1)
                        else:
                            dve.wait_ge(split_steps, 3 * SPLITS * (nxt.n - 1) + SPLITS * 2 + 1)
                    n = P if arg < NC else G * DH
                    bias = bq[:, k, arg:arg + 1] if arg < NC else bk[:, k:k + 1]
                    dve.scalar_tensor_tensor(out=roped[0:n, k, :], in0=ps_misc[0:n, :], scalar=bias,
                                             in1=rope[0:n, int(arg == NC), k, :], op0=ALU.add, op1=ALU.mult) \
                        .then_inc(misc_taken, 1)
                elif step == "v":
                    if nxt.later_than(2):
                        dve.wait_ge(weighed, UB * (nxt.n - 1))
                    dve.tensor_tensor(va[:, nxt.parity], ps_misc[:, :].rearrange("p (j n) -> p j n", j=NT),
                                      bv[:, :].unsqueeze(1).to_broadcast([P, NT, G * 2 * DH]), ALU.add) \
                        .then_inc(misc_taken, 1)
                elif step == "ot":
                    if arg == 0:
                        post.begin(last.n)
                    src = ps_misc[:, :].rearrange("p (h w) -> p h w", h=H)
                    post.did(dve.reciprocal(denom[:, :], src[:, :, DH]))
                    post.settle()
                    dve.tensor_tensor(heads[:, arg, :].rearrange("p (h w) -> p h w", h=H), src[:, :, 0:DH],
                                      denom[:, :].unsqueeze(2).to_broadcast([P, H, DH]), ALU.mult) \
                        .then_inc(misc_taken, 1)
                elif step == "op":
                    dve.tensor_tensor(proj[:, 2 * arg:2 * arg + 2, :],
                                      ps_misc[:, :].rearrange("p (j n) -> p j n", j=2),
                                      bo[:, :].unsqueeze(1).to_broadcast([P, 2, D]), ALU.add) \
                        .then_inc(misc_taken, 1)
                    if arg == 1:
                        dve.wait_ge(misc_taken, misc_number(cur, pos) + 1)
                        layernorm(post, proj, proj, None)
                        post.settle()
                        dve.wait_ge(x_res_loaded, 16 * (last.n + 1))
                        if last.later_than(1):
                            dve.wait_ge(x1_stored, 16 * last.n)
                        dve.tensor_tensor(x1[:, :, :], proj[:, :, :], x_res[:, :, :], ALU.add) \
                            .then_inc(x1_ready, 1)
                        dve.wait_ge(x1_ready, last.n + 1)
                        if last.later_than(1):
                            dve.wait_ge(h2_stored, 16 * last.n)
                        layernorm(post, h2, x1, h2_ready)
                elif step == "rt":
                    dve.tensor_tensor(logits[:, :, :],
                                      ps_misc[:, 0:NT * E].rearrange("p (j e) -> p j e", j=NT),
                                      gate_b[:, :].unsqueeze(1).to_broadcast([P, NT, E]), ALU.add) \
                        .then_inc(misc_taken, 1)
                elif step == "cn":
                    count(cur, pos, last)

            def choose(last):
                dve.wait_ge(gates_exped, last.n + 1)
                post.did(dve.tensor_scalar(gates[:, :, :], gates[:, :, :], 1.0, None, ALU.add))
                post.settle()
                post.did(dve.reciprocal(gates[:, :, :], gates[:, :, :]))
                post.settle()
                pause()
                for j in range(NT):
                    post.did(dve.max(top[:, j, :], gates[:, j, :]))
                post.settle()
                pause()
                for j in range(NT):
                    post.did(dve.max_index(top_at[:, j, :], top[:, j, :], gates[:, j, :]))
                post.did(dve.tensor_tensor(top_sum[:, :], top[:, :, 0], top[:, :, 1], ALU.add))
                post.settle()
                post.did(dve.tensor_copy(expert[:, :, :], top_at[:, :, 0:2]))
                post.did(dve.reciprocal(top_sum[:, :], top_sum[:, :]))
                post.settle()
                post.did(dve.tensor_tensor(routed_w[:, last.n], top[:, :, 0:2],
                                           top_sum[:, :].unsqueeze(2).to_broadcast([P, NT, 2]), ALU.mult))
                post.did(dve.tensor_copy(routed_e[:, last.n], expert[:, :, :]))
                for k in range(2):
                    post.did(dve.tensor_tensor(onehot[:, :, k, :], iota_e[:, :].unsqueeze(1).to_broadcast([P, NT, E]),
                                               expert[:, :, k].unsqueeze(2).to_broadcast([P, NT, E]),
                                               ALU.is_equal))
                post.settle()
                dve.tensor_tensor(chosen[:, :, :], onehot[:, :, 0, :], onehot[:, :, 1, :], ALU.add) \
                    .then_inc(chosen_ready, 1)

            def count(cur, pos, last):
                post.did(dve.tensor_copy(counts[:, 0, :], counts[:, NT, :]))
                for j in range(NT):
                    post.settle()
                    post.did(dve.tensor_tensor(counts[:, j + 1, :], counts[:, j, :],
                                               ps_misc[:, (NT + j) * E:(NT + j + 1) * E], ALU.add))
                post.settle()
                dve.tensor_tensor(place[:, :, :], ps_misc[:, 0:NT * E].rearrange("p (j e) -> p j e", j=NT),
                                  counts[:, 0:NT, :], ALU.add).then_inc(misc_taken, 1)
                dve.wait_ge(misc_taken, misc_number(cur, pos) + 1)
                for k in range(2):
                    post.did(dve.tensor_tensor(placed[:, :, k, :], onehot[:, :, k, :], place[:, :, :], ALU.mult))
                post.settle()
                post.did(dve.tensor_reduce(routed_pos[:, last.n], placed[:, :, :, :], AX_X, ALU.add))
                post.settle()
                if last.later_than(2):
                    dve.wait_ge(scattered[last.parity], 16 * 2 * NT * last.half)
                post.did(dve.tensor_copy(token_i[last.parity][:, :], token[:, :]))
                post.did(dve.tensor_scalar(token[:, :], token[:, :], float(T), None, ALU.add))
                post.settle()
                dve.scalar_tensor_tensor(out=slot[last.parity][:, :, :], in0=expert[:, :, :], scalar=float(TOKENS),
                                         in1=routed_pos[:, last.n], op0=ALU.mult, op1=ALU.add) \
                    .then_inc(slots_ready, 1)
                post.end()

            def body(cur):
                nxt, last = cur.plus(1), cur.plus(-1)
                for n in range(UB):
                    if n == 0 and cur.offset == -1:
                        first_norm(nxt, cur)
                    reduce_max(cur, n)
                    for pos, (at, step, arg) in enumerate(MISC):
                        if at == n and active(cur, step, arg):
                            take(cur, pos)
                    if n == 20 and last.exists:
                        choose(last)
                    if n == 15 and nxt.plus(1).exists:
                        first_norm(nxt.plus(1), cur)

            rounds(dve, body)


POST_STEPS = (NT
              + 2 * (NT + NT + RSQRT_STEPS) + NT
              + 2 + NT + NT + 1 + 2 + 1 + 1 + 2
              + 1 + NT + 2 + 1 + 2)
N_CONSTS = 16
N_LOADS = 13
N_ZEROS = -(-(LIST // 544) // P) + 1


def expert_phases(nc, a, out, v):
    ctx = ExitStack()
    with ctx:
        def sb(name, shape, dt=F32):
            return ctx.enter_context(nc.sbuf_tensor(name, shape, dt))

        def psum(name, shape):
            return ctx.enter_context(nc.psum_tensor(name, shape, F32))

        def sem(name):
            return ctx.enter_context(nc.semaphore(name))

        wgu, wd, ident, counts, iota_e = (v[n] for n in ("wgu", "wd", "ident", "counts", "iota_e"))
        routed_e, routed_pos, routed_w = (v[n] for n in ("routed_e", "routed_pos", "routed_w"))
        id_list, y_dram, h2_dram, x1_dram = (v[n] for n in ("id_list", "y_dram", "h2_dram", "x1_dram"))

        tile_ends = sb("tile_ends", [P, E])
        tiles_of = sb("tiles_of", [P, E])
        tiles_i = sb("tiles_i", [P, E], I32)
        jumps = sb("jumps", [P, E])
        tile_no = sb("tile_no", [1, TILES])
        past = sb("past", [1, TILES, E])
        tile_e = sb("tile_e", [1, TILES])
        tile_at = sb("tile_at", [1, TILES])
        tile_e_i = sb("tile_e_i", [1, TILES], I32)
        tile_at_i = sb("tile_at_i", [1, TILES], I32)
        first_row = sb("first_row", [P, E])
        y_row = sb("y_row", [P, B * NT * 2])
        y_hot = sb("y_hot", [P, B * NT * 2, E])
        y_row_i = sb("y_row_i", [P, B * NT * 2], U32)

        ids = [sb(f"ids{k}", [P, 1], I32) for k in range(8)]
        rows = sb("rows", [P, 8, D])
        rows_t = sb("rows_t", [P, 2, NC, P])
        ex = sb("ex", [P, 2, I])
        hid = sb("hid", [P, 2, I])
        hid_t = sb("hid_t", [P, 2, P])
        ysb = sb("ysb", [P, 2, D])
        y_in = sb("y_in", [P, 4, 2, D])
        y_row_t = [sb(f"y_row_t{k}", [P, 2], U32) for k in range(8)]
        summed = sb("summed", [P, NT, D])
        x1_in = sb("x1_in", [P, NT, D])
        final = sb("final", [P, NT, D])
        stats = sb("stats2", [P, NT, 6])
        moments = sb("moments2", [P, NT, 2])
        rstd = sb("rstd2", [P, NT])
        work = [sb(f"work2{k}", [P, NT]) for k in range(2)]

        ps_t = psum("ps_t", [P, 2, T])
        ps_gu = psum("ps_gu", [P, 2, T])
        ps_ht = psum("ps_ht", [P, 2, T])
        ps_y = psum("ps_y", [P, 2, T])

        plan_steps = sem("plan_steps")
        numbered = sem("numbered")
        plan_ready = sem("plan_ready")
        out_stored = sem("out_stored")

        plan_block = nc.Block()
        block = plan_block.__enter__()

        @block.gpsimd
        def _(pool):
            pool.iota(tile_no[:, :], pattern=[[1, TILES]], base=0, channel_multiplier=0,
                      allow_small_or_imprecise_dtypes=True).then_inc(numbered, 1)

        @block.vector
        def _(dve):
            plan = Steps(dve, plan_steps, 0)
            plan.begin(0)

            def do(ins):
                plan.did(ins)
                plan.settle()

            do(dve.tensor_scalar(tiles_i[:, :], counts[:, NT, :], float(P - 1), None, ALU.add))
            do(dve.tensor_scalar(tiles_i[:, :], tiles_i[:, :], 7, None, ALU.arith_shift_right))
            do(dve.tensor_copy(tiles_of[:, :], tiles_i[:, :]))
            do(dve.tensor_copy(tile_ends[:, 0:1], tiles_of[:, 0:1]))
            for e in range(1, E):
                do(dve.tensor_tensor(tile_ends[:, e:e + 1], tile_ends[:, e - 1:e], tiles_of[:, e:e + 1], ALU.add))
            dve.wait_ge(numbered, 1)
            do(dve.tensor_tensor(past[:, :, :], tile_no[:, :].unsqueeze(2).to_broadcast([1, TILES, E]),
                                 tile_ends[0:1, :].unsqueeze(1).to_broadcast([1, TILES, E]), ALU.is_ge))
            do(dve.tensor_reduce(tile_e[:, :], past[:, :, 0:E - 1], AX_X, ALU.add))
            do(dve.tensor_scalar(jumps[:, :], tiles_of[:, :], -float(P), float(TOKENS), ALU.mult, ALU.add))
            do(dve.tensor_tensor(past[:, :, :], past[:, :, :],
                                 jumps[0:1, :].unsqueeze(1).to_broadcast([1, TILES, E]), ALU.mult))
            do(dve.tensor_reduce(tile_at[:, :], past[:, :, 0:E - 1], AX_X, ALU.add))
            do(dve.scalar_tensor_tensor(out=tile_at[:, :], in0=tile_no[:, :], scalar=float(P), in1=tile_at[:, :],
                                        op0=ALU.mult, op1=ALU.add))
            do(dve.tensor_copy(tile_e_i[:, :], tile_e[:, :]))
            do(dve.tensor_copy(tile_at_i[:, :], tile_at[:, :]))
            do(dve.tensor_tensor(first_row[:, :], tile_ends[:, :], tiles_of[:, :], ALU.subtract))
            do(dve.tensor_scalar(first_row[:, :], first_row[:, :], float(P), None, ALU.mult))
            n = B * NT * 2
            flat = "p b j k -> p (b j k)"
            do(dve.tensor_tensor(y_hot[:, :, :], iota_e[:, :].unsqueeze(1).to_broadcast([P, n, E]),
                                 routed_e[:, :, :, :].rearrange(flat).unsqueeze(2).to_broadcast([P, n, E]),
                                 ALU.is_equal))
            do(dve.tensor_tensor(y_hot[:, :, :], y_hot[:, :, :],
                                 first_row[:, :].unsqueeze(1).to_broadcast([P, n, E]), ALU.mult))
            do(dve.tensor_reduce(y_row[:, :], y_hot[:, :, :], AX_X, ALU.add))
            do(dve.tensor_tensor(y_row[:, :], y_row[:, :], routed_pos[:, :, :, :].rearrange(flat), ALU.add))
            do(dve.tensor_copy(y_row_i[:, :], y_row[:, :]))

        plan_block.__exit__(None, None, None)
        for shared in (False, True):
            mlp_phase(nc, a, out, v, locals(), shared)


def mlp_phase(nc, a, out, v, w, shared):
    wgu, wd, ident = (v[n] for n in ("wgu", "wd", "ident"))
    routed_w, id_list, y_dram, h2_dram, x1_dram = (
        v[n] for n in ("routed_w", "id_list", "y_dram", "h2_dram", "x1_dram"))
    (ids, rows, rows_t, ex, hid, hid_t, ysb, y_in, y_row_t, summed, x1_in, final, stats, moments, rstd, work) = (
        w[n] for n in ("ids", "rows", "rows_t", "ex", "hid", "hid_t", "ysb", "y_in", "y_row_t", "summed",
                       "x1_in", "final", "stats", "moments", "rstd", "work"))
    (ps_t, ps_gu, ps_ht, ps_y, tile_e_i, tile_at_i, y_row_i, out_stored) = (
        w[n] for n in ("ps_t", "ps_gu", "ps_ht", "ps_y", "tile_e_i", "tile_at_i", "y_row_i", "out_stored"))
    tiles = B * NT if shared else TILES
    unroll = 8
    tag = "s" if shared else "r"
    DEPTH = 8
    AHEAD = 5

    ctx = ExitStack()
    with ctx:
        def sem(name):
            return ctx.enter_context(nc.semaphore(f"{name}_{tag}"))

        ids_loaded = [sem(f"ids_loaded{k}") for k in range(DEPTH)]
        rows_loaded = [sem(f"rows_loaded{k}") for k in range(DEPTH)]
        turned, turned_out = sem("turned"), sem("turned_out")
        hidden, gate_exped, hid_steps = sem("hidden"), sem("gate_exped"), sem("hid_steps")
        hid_turned, hid_t_ready = sem("hid_turned"), sem("hid_t_ready")
        y_done, y_taken = sem("y_done"), sem("y_taken")
        y_stored = [sem(f"y_stored{k}") for k in range(2)]
        rows_read = sem("rows_read")
        paused = sem("paused")
        y_row_ready = sem("y_row_ready")
        y_loaded = [sem(f"y_loaded{k}") for k in range(4)]
        x1_loaded = sem("x1_loaded")
        norm_steps, norm_done = sem("norm_steps"), sem("norm_done")
        HID = 4

        class Tile:

            def __init__(self, offset, turn=None):
                self.offset, self.turn = offset, turn
                self.n = offset if turn is None else unroll * turn + offset

            def plus(self, k):
                return Tile(self.offset + k, self.turn)

            @property
            def exists(self):
                return self.turn is not None or 0 <= self.offset < tiles

            def later_than(self, k):
                return self.turn is not None or self.offset >= k

            def buf(self, n):
                return self.offset % n

            def round(self, n):
                return self.offset // n if self.turn is None else (unroll // n) * self.turn + self.offset // n

        def steps_of(eng, body, first=-1, last=2):
            lead = 8
            turns = (tiles - 2 * lead) // unroll
            for k in range(first, lead):
                body(Tile(k))
            with eng.Fori(0, turns) as turn:
                for u in range(unroll):
                    body(Tile(lead + u, turn))
            for k in range(lead + unroll * turns, tiles + last):
                body(Tile(k))

        block = ctx.enter_context(nc.Block())

        @block.sync
        def _(sp):
            if not shared:
                sp.wait_ge(v["h2_stored"], 16 * B)
                sp.wait_ge(v["x1_stored"], 16 * B)
                for k in range(2):
                    sp.wait_ge(v["scattered"][k], 16 * NT * B)

            def load(t):
                k = t.buf(DEPTH)
                if not shared:
                    at = sp.value_load(tile_at_i[0:1, bass.ds(t.n, 1)], min_val=0, max_val=LIST - P)
                    sp.dma_start(ids[k][:, :], id_list[bass.ds(at, P), :]).then_inc(ids_loaded[k], 16)
                else:
                    if t.later_than(DEPTH):
                        sp.wait_ge(rows_read, t.n - DEPTH + 1)
                    sp.dma_start(rows[:, k, :], h2_dram.rearrange("b (j p) d -> (b j) p d", p=P)[t.n]) \
                        .then_inc(rows_loaded[k], 16)

            def store(t):
                if not shared:
                    k = t.buf(2)
                    sp.wait_ge(y_taken, t.n + 1)
                    sp.dma_start(y_dram.rearrange("(n p) d -> n p d", p=P)[t.n], ysb[:, k, :]) \
                        .then_inc(y_stored[k], 16)
                elif t.offset % NT == NT - 1:
                    b = t.round(NT)
                    sp.wait_ge(norm_done, b + 1)
                    sp.dma_start(out[b].rearrange("(j p) d -> p j d", p=P), final[:, :, :]) \
                        .then_inc(out_stored, 16)

            def body(t):
                if t.plus(-3).exists:
                    store(t.plus(-3))
                if t.plus(AHEAD).exists:
                    load(t.plus(AHEAD))
                if shared and t.exists and t.offset % NT == 2:
                    b = t.round(NT)
                    if t.later_than(NT):
                        sp.wait_ge(norm_done, b)
                    sp.dma_start(x1_in[:, :, :], x1_dram[b].rearrange("(j p) d -> p j d", p=P)) \
                        .then_inc(x1_loaded, 16)

            steps_of(sp, body, first=-AHEAD, last=3)
            if shared:
                sp.wait_ge(out_stored, 16 * B)
            else:
                for k in range(2):
                    sp.wait_ge(y_stored[k], 16 * TILES // 2)

        @block.gpsimd
        def _(pool):
            pause = Pause(pool, v["pool_cell"], v["zero_col"][0:1, 0:1], paused)

            def body(t):
                k = t.buf(DEPTH)
                if not t.exists:
                    return
                if not shared:
                    pool.wait_ge(ids_loaded[k], 16 * (t.round(DEPTH) + 1))
                    if t.later_than(DEPTH):
                        pool.wait_ge(turned, t.n - DEPTH + 1)
                    pause(t.n, t.later_than(1))
                    pool.indirect_dma_start(
                        out=rows[:, k, :], out_offset=None, in_=h2_dram.rearrange("b t d -> (b t) d"),
                        in_offset=bass.IndirectOffsetOnAxis(ap=ids[k][:, 0:1].bitcast(U32), axis=0),
                    ).then_inc(rows_loaded[k], 16)
                else:
                    k2 = t.buf(4)
                    pool.wait_ge(y_row_ready, t.n + 1)
                    if t.later_than(4):
                        pool.wait_ge(rows_read, t.n - 3)
                    pause(t.n, t.later_than(1))
                    for c in range(2):
                        pool.indirect_dma_start(
                            out=y_in[:, k2, c, :], out_offset=None, in_=y_dram[:, :],
                            in_offset=bass.IndirectOffsetOnAxis(ap=y_row_t[k][:, c:c + 1], axis=0),
                        ).then_inc(y_loaded[k2], 16)

            steps_of(pool, body)

        @block.tensor
        def _(pe):
            pe.wait_ge(v["experts_in"], 16 * 3 * (E + 1))

            def expert(t):
                if shared:
                    return E
                return pe.value_load(tile_e_i[0:1, bass.ds(t.n, 1)], min_val=0, max_val=E - 1)

            def turn_rows(t):
                pe.wait_ge(rows_loaded[t.buf(DEPTH)], 16 * (t.round(DEPTH) + 1))
                if t.later_than(2):
                    pe.wait_ge(turned_out, t.n - 1)
                for c in range(NC):
                    ins = pe.transpose(ps_t[:, t.buf(2), c * P:(c + 1) * P],
                                       rows[:, t.buf(DEPTH), c * P:(c + 1) * P], ident[:, :])
                ins.then_inc(turned, 1)

            def gate_up(t):
                e = expert(t)
                pe.wait_ge(turned_out, t.n + 1)
                if t.later_than(2):
                    pe.wait_ge(hid_steps, HID * (t.n - 1))
                for c in range(NC):
                    ins = pe.matmul(ps_gu[:, t.buf(2), 0:2 * I], rows_t[:, t.buf(2), c, :], wgu[:, e, c, :],
                                    start=(c == 0), stop=(c == NC - 1))
                ins.then_inc(hidden, 1)

            def turn_hidden(t):
                pe.wait_ge(hid_steps, HID * (t.n + 1))
                if t.later_than(2):
                    pe.wait_ge(hid_t_ready, t.n - 1)
                pe.transpose(ps_ht[:, t.buf(2), 0:P], hid[:, t.buf(2), :], ident[:, :]).then_inc(hid_turned, 1)

            def down(t):
                e = expert(t)
                pe.wait_ge(hid_t_ready, t.n + 1)
                if t.later_than(2):
                    pe.wait_ge(y_taken, t.n - 1)
                pe.matmul(ps_y[:, t.buf(2), 0:D], hid_t[:, t.buf(2), :], wd[:, e, :],
                          start=True, stop=True).then_inc(y_done, 1)

            def body(t):
                if t.plus(-2).exists:
                    turn_hidden(t.plus(-2))
                if t.plus(1).exists:
                    turn_rows(t.plus(1))
                if t.exists:
                    gate_up(t)
                if t.plus(-2).exists:
                    down(t.plus(-2))

            steps_of(pe, body)

        @block.scalar
        def _(act):
            def body(t):
                if t.plus(-2).exists:
                    h = t.plus(-2)
                    act.wait_ge(hid_turned, h.n + 1)
                    if h.later_than(2):
                        act.wait_ge(y_done, h.n - 1)
                    act.copy(hid_t[:, h.buf(2), :], ps_ht[:, h.buf(2), 0:P]).then_inc(hid_t_ready, 1)
                if t.plus(1).exists:
                    r = t.plus(1)
                    act.wait_ge(turned, r.n + 1)
                    if r.later_than(2):
                        act.wait_ge(hidden, r.n - 1)
                    act.copy(rows_t[:, r.buf(2)].rearrange("p c n -> p (c n)"), ps_t[:, r.buf(2), 0:D]) \
                        .then_inc(turned_out, 1)
                if t.exists:
                    act.wait_ge(hidden, t.n + 1)
                    if t.later_than(2):
                        act.wait_ge(hid_steps, HID * (t.n - 1))
                    act.activation(ex[:, t.buf(2), :], ps_gu[:, t.buf(2), 0:I], ACT.Exp, scale=-1.0) \
                        .then_inc(gate_exped, 1)
                if t.plus(-2).exists and not shared:
                    y = t.plus(-2)
                    act.wait_ge(y_done, y.n + 1)
                    if y.later_than(2):
                        act.wait_ge(y_stored[y.buf(2)], 16 * y.round(2))
                    act.copy(ysb[:, y.buf(2), :], ps_y[:, y.buf(2), 0:D]).then_inc(y_taken, 1)

            steps_of(act, body)

        @block.vector
        def _(dve):
            pause = Pause(dve, v["dve_cell"])

            hs = Steps(dve, hid_steps, HID)
            norm = Steps(dve, norm_steps, NT * 2 + NT + RSQRT_STEPS + NT)

            def silu(t):
                k = t.buf(2)
                dve.wait_ge(gate_exped, t.n + 1)
                if t.later_than(2):
                    dve.wait_ge(hid_turned, t.n - 1)
                hs.begin(t.n)
                hs.did(dve.tensor_scalar(ex[:, k, :], ex[:, k, :], 1.0, None, ALU.add))
                hs.settle()
                hs.did(dve.reciprocal(ex[:, k, :], ex[:, k, :]))
                hs.settle()
                hs.did(dve.tensor_tensor(hid[:, k, :], ps_gu[:, k, 0:I], ex[:, k, :], ALU.mult))
                hs.settle()
                hs.did(dve.tensor_tensor(hid[:, k, :], ps_gu[:, k, I:2 * I], hid[:, k, :], ALU.mult))
                hs.end()

            def name_rows(t):
                k = t.buf(8)
                if t.later_than(8):
                    dve.wait_ge(y_loaded[t.buf(4)], 32 * (t.round(4) - 1))
                dve.tensor_copy(y_row_t[k][:, :], y_row_i[:, bass.ds(2 * t.n, 2)]).then_inc(y_row_ready, 1)

            def combine(t):
                j, k2, k4 = t.offset % NT, t.buf(2), t.buf(4)
                b = t.round(NT)
                norm.begin(b)
                norm.c = 2 * j
                dve.wait_ge(y_done, t.n + 1)
                dve.wait_ge(y_loaded[k4], 32 * (t.round(4) + 1))
                s = summed[:, j, :]
                dve.tensor_tensor(s, ps_y[:, k2, 0:D], rows[:, t.buf(DEPTH), :], ALU.add).then_inc(y_taken, 1)
                dve.wait_ge(y_taken, t.n + 1)
                wt = routed_w[:, b, j, :]
                norm.did(dve.scalar_tensor_tensor(out=s, in0=y_in[:, k4, 0, :], scalar=wt[:, 0:1], in1=s,
                                                  op0=ALU.mult, op1=ALU.add))
                norm.settle()
                dve.scalar_tensor_tensor(out=s, in0=y_in[:, k4, 1, :], scalar=wt[:, 1:2], in1=s,
                                         op0=ALU.mult, op1=ALU.add).then_inc(rows_read, 1)
                dve.wait_ge(rows_read, t.n + 1)
                norm.did(dve.bn_stats(stats[:, j, :], s))
                if j == NT - 1:
                    norm.settle()
                    pause()
                    for i in range(NT):
                        norm.did(dve.bn_aggr(moments[:, i, :], stats[:, i, :]))
                    norm.settle()
                    rsqrt(dve, norm, rstd[:, :], moments[:, :, 1], [x[:, :] for x in work])
                    if t.later_than(NT):
                        dve.wait_ge(out_stored, 16 * b)
                    for i in range(NT):
                        norm.did(dve.tensor_scalar(final[:, i, :], summed[:, i, :], moments[:, i, 0:1],
                                                   rstd[:, i:i + 1], ALU.subtract, ALU.mult))
                    norm.settle()
                    norm.end()
                    dve.wait_ge(x1_loaded, 16 * (b + 1))
                    dve.tensor_tensor(final[:, :, :], final[:, :, :], x1_in[:, :, :], ALU.add) \
                        .then_inc(norm_done, 1)

            def body(t):
                if shared and t.plus(3).exists:
                    name_rows(t.plus(3))
                if t.exists:
                    silu(t)
                if shared and t.plus(-2).exists:
                    combine(t.plus(-2))

            steps_of(dve, body, first=-3)


def kernel(**inputs):
    import concourse.bacc as bacc
    from concourse.bass_utils import run_bass_kernel_spmd as run

    x = {k: np.ascontiguousarray(np.asarray(w)) for k, w in inputs.items()}
    f = lambda n: x["L0_" + n]
    swap_q, swap_k = np.arange(D) ^ 1, np.arange(G * DH) ^ 1
    freq = np.exp(-(np.arange(0, DH, 2, dtype=np.float32) / np.float32(DH)) * np.log(np.float32(10000.0)))
    angle = np.arange(T, dtype=np.float32)[:, None] * freq.astype(np.float32)
    row = np.arange(P) % DH
    cos = np.cos(angle).astype(np.float32).T[row // 2]
    sin = np.sin(angle).astype(np.float32).T[row // 2] * np.where(row % 2, 1, -1).astype(np.float32)[:, None]
    scale = np.float32(1 / np.sqrt(DH))
    rope = np.stack([np.stack([cos * scale, sin * scale], 1), np.stack([cos, sin], 1)], 1).astype(np.float32)
    wv = np.zeros((D, G, 2, DH), np.float32)
    wv[:, :, 0] = f("attn_Wv").reshape(D, G, DH)
    bv = np.ones((G, 2, DH), np.float32)
    bv[:, 0] = f("attn_bv").reshape(G, DH)
    arrays = {
        "x": f("attn_x"), "wq0": f("attn_Wq"), "wq1": f("attn_Wq")[:, swap_q], "wk0": f("attn_Wk"),
        "wk1": f("attn_Wk")[:, swap_k],
        "bq": np.stack([f("attn_bq").reshape(NC, P).T, f("attn_bq")[swap_q].reshape(NC, P).T], 1),
        "bk": np.stack([f("attn_bk"), f("attn_bk")[swap_k]], 1),
        "rope": rope, "wv": wv.reshape(D, -1), "bv": bv.reshape(-1), "wo": f("attn_Wo"), "bo": f("attn_bo"),
        "gate_w": f("ffn_gate_w"), "gate_b": f("ffn_gate_b"), "eg": f("ffn_experts_wg"), "eu": f("ffn_experts_wu"),
        "ed": f("ffn_experts_wd"), "sg": f("ffn_shared_wg"), "su": f("ffn_shared_wu"), "sd": f("ffn_shared_wd"),
    }
    nc = bacc.Bacc("TRN2", target_bir_lowering=False, num_devices=1)
    ins = {}
    for k in arrays:
        arrays[k] = np.ascontiguousarray(arrays[k])
        ins[k] = nc.dram_tensor(f"in_{k}", arrays[k].shape, F32, kind="ExternalInput").ap()
    out = nc.dram_tensor("out_0", (B, T, D), F32, kind="ExternalOutput").ap()
    layer(nc, ins, out)
    r = run(nc, [{f"in_{k}": w for k, w in arrays.items()}], core_ids=[0])
    return r.results[0]["out_0"]
```

```python
from contextlib import ExitStack

import numpy as np

import concourse.bass as bass
from concourse import mybir

F32 = mybir.dt.float32
BF16 = mybir.dt.bfloat16
I32 = mybir.dt.int32
U32 = mybir.dt.uint32
ALU = mybir.AluOpType
ACT = mybir.ActivationFunctionType
AX_X = mybir.AxisListType.X

P = 128
B, T, D = 32, 512, 256
NT = T // P
NC = D // P
H, G, DH = 16, 4, 16
HG = H // G
E, I = 16, 128
TOKENS = B * T
PARTS = 3
BLOCKS = [(0, 0), (1, 0), (2, 0), (0, 1), (1, 1), (0, 2)]
KR = len(BLOCKS) * DH
KM = KR + PARTS
MASKED = -3.0e38
EPS = 1e-5
TILES = TOKENS * 2 // P + E
LIST = (E - 1) * TOKENS + TILES * P
RSQRT_SEED = float(0x5F3759DF)

MAX_UNITS = [(0, 0, 4, 128, 128), (1, 0, 4, 256, 256), (2, 0, 2, 384, 512), (2, 2, 2, 384, 512),
             (3, 0, 2, 512, 512), (3, 2, 2, 512, 512)]
EXP_UNITS = [(0, 0, 2, 512, 512), (0, 2, 2, 512, 512), (1, 0, 2, 384, 512), (1, 2, 2, 384, 512),
             (2, 0, 4, 256, 256), (3, 0, 4, 128, 128)]
NU = 6
UB = G * NU
MAX_LEAD = 9

MISC = [(0, "xt", 0), (1, "xt", 1), (2, "ot", 0), (2, "qa", 0), (3, "ot", 1), (3, "qb", 0), (3, "mt", 1),
        (4, "ot", 2), (4, "qa", 1), (5, "ot", 3), (5, "qb", 1), (6, "qa", 2), (7, "qb", 2), (8, "v", 0),
        (9, "at", 0), (9, "mt", 2), (10, "at", 1), (11, "op", 0), (12, "op", 1), (15, "mt", 3),
        (18, "ht", 0), (19, "ht", 1), (20, "rt", 0), (21, "mt", 4), (23, "cn", 0)]
OF_NEXT = ("xt", "qa", "qb", "v")
OF_LAST = ("ot", "at", "op", "ht", "rt", "cn")


class Batch:

    def __init__(self, offset, pair=None):
        self.offset, self.pair = offset, pair
        self.n = offset if pair is None else 2 * pair + offset
        self.parity = offset % 2
        self.half = offset // 2 if pair is None else pair + offset // 2

    def plus(self, k):
        return Batch(self.offset + k, self.pair)

    @property
    def exists(self):
        return self.pair is not None or 0 <= self.offset < B

    def later_than(self, k):
        return self.pair is not None or self.offset >= k


def active(cur, step, arg):
    if step in OF_NEXT:
        return cur.plus(1).exists
    if step in OF_LAST:
        return cur.plus(-1).exists
    return cur.plus(arg // G).exists


def fills(cur):
    return sum(active(cur, s, a) for _, s, a in MISC)


def misc_number(cur, pos):
    before = sum(active(cur, s, a) for _, s, a in MISC[:pos])
    if cur.pair is None:
        return sum(fills(Batch(k)) for k in range(-1, cur.offset)) + before
    return sum(fills(Batch(k)) for k in (-1, 0)) + len(MISC) * (cur.n - 1) + before


def position(step, arg):
    return [m[1:] for m in MISC].index((step, arg))


def rounds(eng, body):
    for k in range(-1, 3):
        body(Batch(k))
    with eng.Fori(0, (B - 6) // 2) as pair:
        for u in (3, 4):
            body(Batch(u, pair))
    for k in range(B - 3, B + 1):
        body(Batch(k))


class Pause:

    def __init__(self, eng, cell, zeros=None, done=None):
        self.eng, self.cell, self.zeros, self.done = eng, cell[:, 0:1], zeros, done

    def __call__(self, number=None, later=False):
        if self.done is None:
            self.eng.memset(self.cell, 0.0)
            return
        if later:
            self.eng.wait_ge(self.done, number)
        self.eng.tensor_tensor(self.cell, self.zeros, self.zeros, ALU.add).then_inc(self.done, 1)


def wait_all(eng, *waits):
    values = [v if isinstance(v, int) else eng.snap(v) for _, v in waits]
    for (sem, _), v in zip(waits, values):
        eng.wait_ge(sem, v)


class Steps:

    def __init__(self, eng, sem, per):
        self.eng, self.sem, self.per = eng, sem, per

    def begin(self, n):
        self.base, self.c = self.per * n, 0

    def did(self, ins):
        ins.then_inc(self.sem, 1)
        self.c += 1

    def settle(self):
        self.eng.wait_ge(self.sem, self.base + self.c)

    def end(self):
        assert self.c == self.per, (self.c, self.per)


RSQRT_STEPS = 13


def rsqrt(dve, steps, out, var, work):
    steps.did(dve.tensor_scalar(work[0], var, EPS, None, ALU.add))
    steps.settle()
    steps.did(dve.tensor_scalar(out.bitcast(I32), work[0].bitcast(I32), 1, None, ALU.arith_shift_right))
    steps.did(dve.tensor_scalar(work[1], work[0], -0.5, None, ALU.mult))
    steps.settle()
    steps.did(dve.tensor_scalar(out.bitcast(I32), out.bitcast(I32), -1.0, RSQRT_SEED, ALU.mult, ALU.add))
    steps.settle()
    for _ in range(3):
        steps.did(dve.tensor_tensor(work[0], out, out, ALU.mult))
        steps.settle()
        steps.did(dve.tensor_tensor(work[0], work[0], work[1], ALU.mult))
        steps.settle()
        steps.did(dve.scalar_tensor_tensor(out=out, in0=work[0], scalar=1.5, in1=out, op0=ALU.add, op1=ALU.mult))
        steps.settle()


def layer(nc, a, out):
    ctx = ExitStack()
    with ctx:
        def sb(name, shape, dt=F32):
            return ctx.enter_context(nc.sbuf_tensor(name, shape, dt))

        def sem(name):
            return ctx.enter_context(nc.semaphore(name))

        def dram(name, shape, dt=F32):
            return nc.dram_tensor(name, shape, dt, kind="Internal").ap()

        q_parts_dram = dram("q_parts_dram", [2, H, PARTS, DH, T], BF16)
        k_parts_dram = dram("k_parts_dram", [2, G, PARTS, DH, T], BF16)
        x1_dram = dram("x1_dram", [B, T, D])
        h2_dram = dram("h2_dram", [B, T, D])
        id_list = dram("id_list", [LIST, 1], I32)
        y_dram = dram("y_dram", [TILES * P, D])

        wq = sb("wq", [P, 2, NC, D])
        wk = sb("wk", [P, 2, NC, G * DH])
        bq = sb("bq", [P, 2, NC])
        bk = sb("bk", [G * DH, 2])
        rope = sb("rope", [P, 2, 2, T])
        wv = sb("wv", [P, NC, G * 2 * DH])
        bv = sb("bv", [P, G * 2 * DH])
        wo = sb("wo", [P, NC, D])
        bo = sb("bo", [P, D])
        gate_w = sb("gate_w", [P, NC, E])
        gate_b = sb("gate_b", [P, E])
        wgu = sb("wgu", [P, E + 1, NC, 2 * I])
        wd = sb("wd", [P, E + 1, D])
        ident = sb("ident", [P, P])
        ident_bf = sb("ident_bf", [P, P], BF16)
        mask_max = sb("mask_max", [P, P], BF16)
        mask_exp = sb("mask_exp", [P, P], BF16)
        before = sb("before", [P, P], BF16)
        ones_bf = sb("ones_bf", [P, P], BF16)
        iota_e = sb("iota_e", [P, E])
        token = sb("token", [P, NT])
        zeros = sb("zeros", [P, 544], I32)
        routed_e = sb("routed_e", [P, B, NT, 2])
        routed_pos = sb("routed_pos", [P, B, NT, 2])
        routed_w = sb("routed_w", [P, B, NT, 2])
        counts = sb("counts", [P, NT + 1, E])

        pool_cell, dve_cell = sb("pool_cell", [1, 2]), sb("dve_cell", [1, 2])
        zero_col = sb("zero_col", [P, 1])

        weights_in = sem("weights_in")
        consts = sem("consts")
        zeroed = sem("zeroed")
        experts_in = sem("experts_in")
        x1_stored, h2_stored = sem("x1_stored"), sem("h2_stored")
        scattered = [sem(f"scattered{k}") for k in range(2)]

        attention_phase(nc, a, locals())
        expert_phases(nc, a, out, locals())


def attention_phase(nc, a, v):
    (q_parts_dram, k_parts_dram, x1_dram, h2_dram, id_list) = (
        v[n] for n in ("q_parts_dram", "k_parts_dram", "x1_dram", "h2_dram", "id_list"))
    (wq, wk, bq, bk, rope, wv, bv, wo, bo, gate_w, gate_b, wgu, wd) = (
        v[n] for n in ("wq", "wk", "bq", "bk", "rope", "wv", "bv", "wo", "bo", "gate_w", "gate_b", "wgu", "wd"))
    (ident, ident_bf, mask_max, mask_exp, before, ones_bf, iota_e, token, zeros) = (
        v[n] for n in ("ident", "ident_bf", "mask_max", "mask_exp", "before", "ones_bf", "iota_e", "token",
                       "zeros"))
    (routed_e, routed_pos, routed_w, counts, pool_cell, dve_cell, zero_col) = (
        v[n] for n in ("routed_e", "routed_pos", "routed_w", "counts", "pool_cell", "dve_cell", "zero_col"))
    (weights_in, experts_in, consts, zeroed, x1_stored, h2_stored, scattered) = (
        v[n] for n in ("weights_in", "experts_in", "consts", "zeroed", "x1_stored", "h2_stored", "scattered"))

    ctx = ExitStack()
    with ctx:
        def sb(name, shape, dt=F32):
            return ctx.enter_context(nc.sbuf_tensor(name, shape, dt))

        def psum(name, shape):
            return ctx.enter_context(nc.psum_tensor(name, shape, F32))

        def sem(name):
            return ctx.enter_context(nc.semaphore(name))

        x_in = sb("x_in", [P, 2, NT, D])
        h1 = sb("h1", [P, NT, D])
        h1t = sb("h1t", [P, NC, T])
        roped = sb("roped", [P, 2, 2, T])
        rest = sb("rest", [P, T])
        q_parts = sb("q_parts", [P, NC, PARTS, T], BF16)
        k_parts = sb("k_parts", [G * DH, PARTS, T], BF16)
        qs = sb("qs", [P, 2, H, T], BF16)
        ks = sb("ks", [P, 2, G, T], BF16)
        va = sb("va", [P, 2, NT, G * 2 * DH])
        negmax = sb("negmax", [P, 2, NT, HG])
        negmax_rest = sb("negmax_rest", [P, NT, HG])
        negmax_parts = sb("negmax_parts", [P, 2, NT, PARTS, HG], BF16)
        negmax_t = sb("negmax_t", [PARTS * HG, T], BF16)
        probs = sb("probs", [P, 2, 2 * T])
        heads_t = sb("heads_t", [P, G, T])
        denom = sb("denom", [P, H])
        heads = sb("heads", [P, NT, D])
        headst = sb("headst", [P, NC, T])
        proj = sb("proj", [P, NT, D])
        x_res = sb("x_res", [P, NT, D])
        x1 = sb("x1", [P, NT, D])
        h2 = sb("h2", [P, NT, D])
        h2t = sb("h2t", [P, NC, T])
        stats = sb("stats", [P, NT, 6])
        moments = sb("moments", [P, NT, 2])
        rstd = sb("rstd", [P, NT])
        work = [sb(f"work{k}", [P, NT]) for k in range(2)]
        logits = sb("logits", [P, NT, E])
        gates = sb("gates", [P, NT, E])
        top = sb("top", [P, NT, 8])
        top_at = sb("top_at", [P, NT, 8], U32)
        expert = sb("expert", [P, NT, 2])
        top_sum = sb("top_sum", [P, NT])
        onehot = sb("onehot", [P, NT, 2, E])
        chosen = sb("chosen", [P, NT, E], BF16)
        place = sb("place", [P, NT, E])
        placed = sb("placed", [P, NT, 2, E])
        slot = [sb(f"slot{k}", [P, NT, 2], U32) for k in range(2)]
        token_i = [sb(f"token_i{k}", [P, NT], I32) for k in range(2)]

        ps_exp = psum("ps_exp", [P, 2, 2 * T])
        ps_max = psum("ps_max", [P, 2 * T])
        ps_out = psum("ps_out", [P, T])
        ps_misc = psum("ps_misc", [P, T])

        x_loaded = [sem(f"x_loaded{k}") for k in range(2)]
        x_res_loaded = sem("x_res_loaded")
        stack_ones = sem("stack_ones")
        paused = sem("paused")
        ln1_steps = sem("ln1_steps")
        h1_ready = sem("h1_ready")
        misc_full, misc_taken = sem("misc_full"), sem("misc_taken")
        split_steps = sem("split_steps")
        parts_stored = [sem(f"parts_stored{k}") for k in range(2)]
        stacks_loaded = [sem(f"stacks_loaded{k}") for k in range(2)]
        max_scored, max_reduced = sem("max_scored"), sem("max_reduced")
        negmax_steps = sem("negmax_steps")
        negmax_loaded = [sem(f"negmax_loaded{k}") for k in range(2)]
        scored, exped, weighed = sem("scored"), sem("exped"), sem("weighed")
        heads_t_ready = sem("heads_t_ready")
        post_steps = sem("post_steps")
        x1_ready, h2_ready = sem("x1_ready"), sem("h2_ready")
        gates_exped = sem("gates_exped")
        chosen_ready = sem("chosen_ready")
        slots_ready = sem("slots_ready")

        n_weights = 0
        SPLITS = 5
        PER_STORE = 16 * 3 * PARTS
        Q_LOADS = [(0, 3, 0), (3 * DH, 2, 0), (5 * DH, 1, 0)]
        PER_LOAD = 16 * (len(Q_LOADS) + len(BLOCKS))

        def wait_misc(eng, cur, step, arg):
            eng.wait_ge(misc_full, misc_number(cur, position(step, arg)) + 1)

        def max_unit(cur, n):
            m = n + MAX_LEAD
            b = cur.plus(m // UB)
            return b, (m % UB) // NU, m % NU

        block = ctx.enter_context(nc.Block())

        @block.sync
        def _(sp):
            loads = [(wq[:, k], a[f"wq{k}"].rearrange("(c p) n -> p c n", p=P)) for k in range(2)]
            loads += [(wk[:, k], a[f"wk{k}"].rearrange("(c p) n -> p c n", p=P)) for k in range(2)]
            loads += [(bq[:, :, :], a["bq"]), (bk[:, :], a["bk"]), (rope[:, :, :, :], a["rope"]),
                      (wv[:, :, :], a["wv"].rearrange("(c p) n -> p c n", p=P)),
                      (bv[:, :], a["bv"].partition_broadcast(P)), (bo[:, :], a["bo"].partition_broadcast(P)),
                      (wo[:, :, :], a["wo"].rearrange("(c p) n -> p c n", p=P)),
                      (gate_w[:, :, :], a["gate_w"].rearrange("(c p) n -> p c n", p=P)),
                      (gate_b[:, :], a["gate_b"].partition_broadcast(P))]
            sp.dma_start(x_in[:, 0], a["x"][0].rearrange("(j p) d -> p j d", p=P)).then_inc(x_loaded[0], 16)
            for dst, src in loads:
                sp.dma_start(dst, src).then_inc(weights_in, 16)
            assert len(loads) == N_LOADS
            sp.wait_ge(consts, N_CONSTS)
            rows = LIST // 544
            done = 0
            while done < rows:
                k = min(P, rows - done)
                sp.dma_start(id_list[done * 544:(done + k) * 544].rearrange("(p n) o -> p (n o)", p=k),
                             zeros[0:k, :]).then_inc(zeroed, 16)
                done += k
            sp.dma_start(id_list[rows * 544:LIST].rearrange("n o -> o n"), zeros[0:1, 0:LIST - rows * 544]) \
                .then_inc(zeroed, 16)
            for e in range(E):
                sp.dma_start(wgu[:, e, :, 0:I], a["eg"][e].rearrange("(c p) n -> p c n", p=P)).then_inc(experts_in, 16)
                sp.dma_start(wgu[:, e, :, I:], a["eu"][e].rearrange("(c p) n -> p c n", p=P)).then_inc(experts_in, 16)
                sp.dma_start(wd[:, e, :], a["ed"][e]).then_inc(experts_in, 16)
            sp.dma_start(wgu[:, E, :, 0:I], a["sg"].rearrange("(c p) n -> p c n", p=P)).then_inc(experts_in, 16)
            sp.dma_start(wgu[:, E, :, I:], a["su"].rearrange("(c p) n -> p c n", p=P)).then_inc(experts_in, 16)
            sp.dma_start(wd[:, E, :], a["sd"]).then_inc(experts_in, 16)

            def store_parts(nxt, unit):
                waits = [(split_steps, 3 * SPLITS * nxt.n + SPLITS * (unit + 1))]
                if unit == 0 and nxt.later_than(2):
                    waits.append((stacks_loaded[nxt.parity], PER_LOAD * nxt.half))
                wait_all(sp, *waits)
                for part in range(PARTS):
                    if unit < NC:
                        hs = slice(unit * H // NC, (unit + 1) * H // NC)
                        sp.dma_start(q_parts_dram[nxt.parity, hs, part], q_parts[:, unit, part, :]) \
                            .then_inc(parts_stored[nxt.parity], 16)
                    else:
                        sp.dma_start(k_parts_dram[nxt.parity, :, part], k_parts[:, part, :]) \
                            .then_inc(parts_stored[nxt.parity], 16)

            def load_stacks(nxt):
                sp.wait_ge(parts_stored[nxt.parity], PER_STORE * (nxt.half + 1))
                src = q_parts_dram[nxt.parity]
                for row, n, first in Q_LOADS:
                    sp.dma_start(qs[row:row + n * DH, nxt.parity],
                                 src[:, first:first + n].rearrange("h a d t -> (a d) h t")) \
                        .then_inc(stacks_loaded[nxt.parity], 16)
                for k, (_, part) in enumerate(BLOCKS):
                    sp.dma_start(ks[k * DH:(k + 1) * DH, nxt.parity],
                                 k_parts_dram[nxt.parity, :, part].rearrange("g d t -> d g t")) \
                        .then_inc(stacks_loaded[nxt.parity], 16)

            def load_negmax(cur, pos, b, g):
                sp.wait_ge(misc_taken, misc_number(cur, pos) + 1)
                for part in range(PARTS):
                    sp.dma_start(qs[KR + part:KR + part + 1, b.parity, g * HG:(g + 1) * HG, :],
                                 negmax_t[part * HG:(part + 1) * HG, :]).then_inc(negmax_loaded[g % 2], 16)

            def body(cur):
                nxt, last = cur.plus(1), cur.plus(-1)
                for n in range(UB):
                    if n == 0 and nxt.plus(1).exists:
                        after = nxt.plus(1)
                        if after.later_than(2):
                            sp.wait_ge(h1_ready, after.n - 1)
                        sp.dma_start(x_in[:, after.parity], a["x"][after.n].rearrange("(j p) d -> p j d", p=P)) \
                            .then_inc(x_loaded[after.parity], 16)
                    if n == 1 and last.exists:
                        if last.later_than(1):
                            sp.wait_ge(x1_ready, last.n)
                        sp.dma_start(x_res[:, :, :], a["x"][last.n].rearrange("(j p) d -> p j d", p=P)) \
                            .then_inc(x_res_loaded, 16)
                    if nxt.exists and n in (6, 8, 10):
                        store_parts(nxt, (n - 6) // 2)
                    if nxt.exists and n == 12:
                        load_stacks(nxt)
                    if n == 17 and last.exists:
                        sp.wait_ge(x1_ready, last.n + 1)
                        sp.dma_start(x1_dram[last.n].rearrange("(j p) d -> p j d", p=P), x1[:, :, :]) \
                            .then_inc(x1_stored, 16)
                    if n == 19 and last.exists:
                        sp.wait_ge(h2_ready, last.n + 1)
                        sp.dma_start(h2_dram[last.n].rearrange("(j p) d -> p j d", p=P), h2[:, :, :]) \
                            .then_inc(h2_stored, 16)
                    for pos, (at, step, g) in enumerate(MISC):
                        if at == n and step == "mt" and active(cur, step, g):
                            load_negmax(cur, pos, cur.plus(g // G), g % G)

            rounds(sp, body)

        @block.gpsimd
        def _(pool):
            pause = Pause(pool, pool_cell, zero_col[0:1, 0:1], paused)

            pool.memset(ident[:, :], 0.0).then_inc(consts, 1)
            pool.memset(ident_bf[:, :], 0.0).then_inc(consts, 1)
            pool.memset(mask_max[:, :], 0.0).then_inc(consts, 1)
            pool.memset(mask_exp[:, :], 0.0).then_inc(consts, 1)
            pool.memset(before[:, :], 0.0).then_inc(consts, 1)
            pool.memset(ones_bf[:, :], 1.0).then_inc(consts, 1)
            pool.memset(zeros[:, :], 0).then_inc(consts, 1)
            pool.memset(zero_col[:, :], 0.0).then_inc(consts, 1)
            pool.memset(counts[:, NT, :], 0.0).then_inc(consts, 1)
            pool.wait_ge(consts, 9)
            for m in (ident, ident_bf):
                pool.affine_select(out=m[:, :], in_=m[:, :], compare_op=ALU.not_equal, fill=1.0, base=0,
                                   pattern=[[-1, P]], channel_multiplier=1).then_inc(consts, 1)
            pool.affine_select(out=mask_max[:, :], in_=mask_max[:, :], compare_op=ALU.is_ge, fill=MASKED,
                               base=0, pattern=[[-1, P]], channel_multiplier=1).then_inc(consts, 1)
            pool.affine_select(out=mask_exp[:, :], in_=mask_exp[:, :], compare_op=ALU.is_ge, fill=MASKED,
                               base=0, pattern=[[1, P]], channel_multiplier=-1).then_inc(consts, 1)
            pool.affine_select(out=before[:, :], in_=before[:, :], compare_op=ALU.is_ge, fill=1.0,
                               base=0, pattern=[[-1, P]], channel_multiplier=1).then_inc(consts, 1)
            pool.iota(iota_e[:, :], pattern=[[1, E]], base=0, channel_multiplier=0,
                      allow_small_or_imprecise_dtypes=True).then_inc(consts, 1)
            pool.iota(token[:, :], pattern=[[P, NT]], base=0, channel_multiplier=1,
                      allow_small_or_imprecise_dtypes=True).then_inc(consts, 1)

            def split(cur, unit):
                nxt = cur.plus(1)
                n = G * DH if unit == NC else P
                parts = [k_parts[:, k, :] if unit == NC else q_parts[:, unit, k, :] for k in range(PARTS)]
                pool.wait_ge(misc_taken, misc_number(cur, position("qb", unit)) + 1)
                steps = Steps(pool, split_steps, 3 * SPLITS)
                steps.begin(nxt.n)
                steps.c = SPLITS * unit
                r = rest[0:n, :]
                if unit or nxt.later_than(1):
                    steps.settle()
                turn = (nxt.parity + unit) % 2
                steps.did(pool.tensor_tensor(r, roped[0:n, turn, 0, :], roped[0:n, turn, 1, :], ALU.add))
                if unit == 0 and nxt.later_than(1):
                    b = nxt.plus(-1)
                    pool.wait_ge(parts_stored[b.parity], PER_STORE * (b.half + 1))
                for k in range(PARTS):
                    if k == PARTS - 1:
                        break
                    steps.settle()
                    steps.did(pool.tensor_tensor(parts[k], r, zero_col[0:n, :].to_broadcast([n, T]), ALU.add))
                    steps.settle()
                    steps.did(pool.tensor_tensor(parts[2] if k == 1 else r, r, parts[k], ALU.subtract))

            def scatter(last):
                pool.wait_ge(slots_ready, last.n + 1)
                pause(last.n, last.later_than(1))
                for j in range(NT):
                    for k in range(2):
                        pool.indirect_dma_start(
                            out=id_list[:, :], in_=token_i[last.parity][:, j:j + 1], in_offset=None,
                            out_offset=bass.IndirectOffsetOnAxis(ap=slot[last.parity][:, j, k:k + 1], axis=0),
                        ).then_inc(scattered[last.parity], 16)

            def body(cur):
                if cur.plus(1).exists:
                    for unit in range(NC + 1):
                        split(cur, unit)
                if cur.plus(-2).exists:
                    scatter(cur.plus(-2))
                if cur.pair is None and cur.offset == 0:
                    pool.wait_ge(zeroed, 16 * N_ZEROS)

            rounds(pool, body)
            scatter(Batch(B - 1))

        @block.tensor
        def _(pe):
            pe.wait_ge(weights_in, 16 * N_LOADS)
            pe.wait_ge(stack_ones, 1)
            pe.wait_ge(consts, N_CONSTS)

            def misc(cur, pos):
                _, step, arg = MISC[pos]
                nxt, last = cur.plus(1), cur.plus(-1)
                number = misc_number(cur, pos)
                if cur.offset > -1 or pos > 0:
                    pe.wait_ge(misc_taken, number)
                if step == "xt":
                    pe.wait_ge(h1_ready, nxt.n + 1)
                    for j in range(NT):
                        ins = pe.transpose(ps_misc[:, j * P:(j + 1) * P], h1[:, j, arg * P:(arg + 1) * P],
                                           ident[:, :])
                elif step in ("qa", "qb"):
                    k = step == "qb"
                    for c in range(NC):
                        if arg < NC:
                            ins = pe.matmul(ps_misc[:, :], wq[:, k, c, arg * P:(arg + 1) * P], h1t[:, c, :],
                                            start=(c == 0), stop=(c == NC - 1))
                        else:
                            ins = pe.matmul(ps_misc[0:G * DH, :], wk[:, k, c, :], h1t[:, c, :],
                                            start=(c == 0), stop=(c == NC - 1))
                elif step == "v":
                    for j in range(NT):
                        for c in range(NC):
                            ins = pe.matmul(ps_misc[:, j * P:(j + 1) * P], h1t[:, c, j * P:(j + 1) * P],
                                            wv[:, c, :], start=(c == 0), stop=(c == NC - 1))
                elif step == "mt":
                    b, g = cur.plus(arg // G), arg % G
                    pe.wait_ge(negmax_steps, 4 * (G * b.n + g + 1))
                    for j in range(NT):
                        ins = pe.transpose(ps_misc[:, :].bitcast(BF16)[0:PARTS * HG, j * P:(j + 1) * P],
                                           negmax_parts[:, g % 2, j].rearrange("p a h -> p (a h)"), ident_bf[:, :])
                elif step == "ot":
                    pe.wait_ge(heads_t_ready, G * (last.n + 1))
                    for g in range(G):
                        ins = pe.transpose(ps_misc[:, g * P:(g + 1) * P], heads_t[:, g, arg * P:(arg + 1) * P],
                                           ident[:, :])
                elif step == "at":
                    for j in range(NT):
                        ins = pe.transpose(ps_misc[:, j * P:(j + 1) * P], heads[:, j, arg * P:(arg + 1) * P],
                                           ident[:, :])
                elif step == "op":
                    for k in range(2):
                        j = 2 * arg + k
                        for c in range(NC):
                            ins = pe.matmul(ps_misc[:, k * D:(k + 1) * D], headst[:, c, j * P:(j + 1) * P],
                                            wo[:, c, :], start=(c == 0), stop=(c == NC - 1))
                elif step == "ht":
                    pe.wait_ge(h2_ready, last.n + 1)
                    for j in range(NT):
                        ins = pe.transpose(ps_misc[:, j * P:(j + 1) * P], h2[:, j, arg * P:(arg + 1) * P],
                                           ident[:, :])
                elif step == "rt":
                    for j in range(NT):
                        for c in range(NC):
                            ins = pe.matmul(ps_misc[:, j * E:(j + 1) * E], h2t[:, c, j * P:(j + 1) * P],
                                            gate_w[:, c, :], start=(c == 0), stop=(c == NC - 1))
                elif step == "cn":
                    pe.wait_ge(chosen_ready, last.n + 1)
                    m = chosen[:, :, :].rearrange("p j e -> p (j e)")
                    pe.matmul(ps_misc[:, 0:NT * E], before[:, :], m, start=True, stop=True)
                    ins = pe.matmul(ps_misc[:, NT * E:2 * NT * E], ones_bf[:, :], m, start=True, stop=True)
                ins.then_inc(misc_full, 1)

            def score_max(cur, n):
                b, g, u = max_unit(cur, n)
                if not b.exists:
                    return
                j, h0, nh, width, stride = MAX_UNITS[u]
                if g == 0 and u == 0:
                    pe.wait_ge(stacks_loaded[b.parity], PER_LOAD * (b.half + 1))
                number = UB * b.n + NU * g + u
                if b.pair is not None or number > 0:
                    pe.wait_ge(max_reduced, number)
                for k in range(nh):
                    h = g * HG + h0 + k
                    at = k * stride
                    pe.matmul(ps_max[:, at:at + width], qs[0:KR, b.parity, h, j * P:(j + 1) * P],
                              ks[0:KR, b.parity, g, 0:width], start=True, stop=False)
                    ins = pe.matmul(ps_max[:, at + j * P:at + (j + 1) * P], ident_bf[:, :], mask_max[:, :],
                                    start=False, stop=True)
                ins.then_inc(max_scored, 1)

            def score_exp(b, n):
                g, u = n // NU, n % NU
                j, h0, nh, width, stride = EXP_UNITS[u]
                if u == 0:
                    pe.wait_ge(negmax_loaded[g % 2], 16 * PARTS * (2 * b.n + g // 2 + 1))
                if b.later_than(1) or n >= 2:
                    pe.wait_ge(exped, UB * b.n + n - 1)
                for k in range(nh):
                    at = k * stride
                    pe.matmul(ps_exp[:, n % 2, at:at + width], ks[0:KM, b.parity, g, j * P:(j + 1) * P],
                              qs[0:KM, b.parity, g * HG + h0 + k, j * P:T], start=True, stop=False)
                    ins = pe.matmul(ps_exp[:, n % 2, at:at + P], ident_bf[:, :], mask_exp[:, :],
                                    start=False, stop=True)
                ins.then_inc(scored, 1)

            def weigh(b, n):
                g, u = n // NU, n % NU
                j, h0, nh, width, stride = EXP_UNITS[u]
                pe.wait_ge(exped, UB * b.n + n + 1)
                if u == 0 and (b.later_than(1) or g > 0):
                    pe.wait_ge(heads_t_ready, G * b.n + g)
                for k in range(nh):
                    hh = h0 + k
                    ins = pe.matmul(ps_out[32 * hh:32 * hh + 32, j * P:T], va[:, b.parity, j, g * 32:(g + 1) * 32],
                                    probs[:, n % 2, k * stride:k * stride + width],
                                    start=(j == 0), stop=(j == NT - 1))
                ins.then_inc(weighed, 1)

            def body(cur):
                for n in range(UB):
                    if cur.exists:
                        score_exp(cur, n)
                    score_max(cur, n)
                    for pos, (at, step, arg) in enumerate(MISC):
                        if at == n and active(cur, step, arg):
                            misc(cur, pos)
                    if n > 0 and cur.exists:
                        weigh(cur, n - 1)
                    if n == 0 and cur.plus(-1).exists:
                        weigh(cur.plus(-1), UB - 1)

            rounds(pe, body)

        @block.scalar
        def _(act):
            def exp(b, n):
                j, h0, nh, width, stride = EXP_UNITS[n % NU]
                act.wait_ge(scored, UB * b.n + n + 1)
                if b.later_than(1) or n >= 2:
                    act.wait_ge(weighed, UB * b.n + n - 1)
                src = ps_exp[:, n % 2, 0:nh * stride].rearrange("p (h w) -> p h w", h=nh)[:, :, 0:width]
                dst = probs[:, n % 2, 0:nh * stride].rearrange("p (h w) -> p h w", h=nh)[:, :, 0:width]
                act.activation(dst, src, ACT.Exp).then_inc(exped, 1)

            def take(cur, pos):
                _, step, arg = MISC[pos]
                if step not in ("xt", "mt", "at", "ht"):
                    return
                nxt, last = cur.plus(1), cur.plus(-1)
                wait_misc(act, cur, step, arg)
                if step == "mt":
                    b, g = cur.plus(arg // G), arg % G
                    if b.pair is not None or b.offset > 0 or g > 0:
                        act.wait_ge(negmax_loaded[(g + 1) % 2],
                                    16 * PARTS * (2 * b.n + (g + 1) // 2))
                    act.copy(negmax_t[:, :], ps_misc[:, :].bitcast(BF16)[0:PARTS * HG, 0:T]) \
                        .then_inc(misc_taken, 1)
                else:
                    dst = {"xt": h1t, "at": headst, "ht": h2t}[step]
                    act.copy(dst[:, arg, :], ps_misc[:, :]).then_inc(misc_taken, 1)

            def body(cur):
                last = cur.plus(-1)
                for n in range(UB):
                    if cur.exists:
                        exp(cur, n)
                    for pos, (at, step, arg) in enumerate(MISC):
                        if at == n and active(cur, step, arg):
                            take(cur, pos)
                    if n == 20 and last.exists:
                        act.wait_ge(misc_taken, misc_number(cur, position("rt", 0)) + 1)
                        act.activation(gates[:, :, :], logits[:, :, :], ACT.Exp, scale=-1.0) \
                            .then_inc(gates_exped, 1)
                    if n % NU == 0:
                        b, g = (cur, n // NU - 1) if n else (last, G - 1)
                        if b.exists:
                            act.wait_ge(weighed, UB * b.n + NU * (g + 1))
                            if g == 0 and b.later_than(1):
                                act.wait_ge(misc_full, misc_number(b, position("ot", NT - 1)) + 1)
                            act.copy(heads_t[:, g, :], ps_out[:, :]).then_inc(heads_t_ready, 1)

            rounds(act, body)

        @block.vector
        def _(dve):
            pause = Pause(dve, dve_cell)

            dve.memset(ks[KR:P, :, :, :], 1.0).then_inc(stack_ones, 1)
            dve.wait_ge(weights_in, 16 * N_LOADS)
            dve.wait_ge(consts, N_CONSTS)
            ln = Steps(dve, ln1_steps, NT + NT + RSQRT_STEPS)
            post = Steps(dve, post_steps, POST_STEPS)

            def moments_of(steps, src):
                for j in range(NT):
                    steps.did(dve.bn_stats(stats[:, j, :], src[:, j, :]))
                steps.settle()
                pause()
                for j in range(NT):
                    steps.did(dve.bn_aggr(moments[:, j, :], stats[:, j, :]))

            def normalise(steps, dst, src, last_sem):
                steps.settle()
                rsqrt(dve, steps, rstd[:, :], moments[:, :, 1], [w[:, :] for w in work])
                for j in range(NT):
                    ins = dve.tensor_scalar(dst[:, j, :], src[:, j, :], moments[:, j, 0:1], rstd[:, j:j + 1],
                                            ALU.subtract, ALU.mult)
                    if last_sem is None:
                        steps.did(ins)
                if last_sem is not None:
                    ins.then_inc(last_sem, 1)

            def first_moments(nxt):
                ln.begin(nxt.n)
                dve.wait_ge(x_loaded[nxt.parity], 16 * (nxt.half + 1))
                moments_of(ln, x_in[:, nxt.parity])

            def first_normalise(nxt):
                normalise(ln, h1, x_in[:, nxt.parity], h1_ready)
                ln.end()

            def add_residual(last):
                post.settle()
                dve.wait_ge(x_res_loaded, 16 * (last.n + 1))
                if last.later_than(1):
                    dve.wait_ge(x1_stored, 16 * last.n)
                dve.tensor_tensor(x1[:, :, :], proj[:, :, :], x_res[:, :, :], ALU.add).then_inc(x1_ready, 1)
                dve.wait_ge(x1_ready, last.n + 1)
                moments_of(post, x1)

            def second_normalise(last):
                if last.later_than(1):
                    dve.wait_ge(h2_stored, 16 * last.n)
                normalise(post, h2, x1, h2_ready)

            def reduce_max(cur, n):
                b, g, u = max_unit(cur, n)
                if not b.exists:
                    return
                j, h0, nh, width, stride = MAX_UNITS[u]
                dve.wait_ge(max_scored, UB * b.n + NU * g + u + 1)
                src = ps_max[:, 0:nh * stride].rearrange("p (h w) -> p h w", h=nh)[:, :, 0:width]
                dve.tensor_reduce(negmax[:, g % 2, j, h0:h0 + nh], src, AX_X, ALU.max, negate=True) \
                    .then_inc(max_reduced, 1)
                if u == NU - 1:
                    dve.wait_ge(max_reduced, UB * b.n + NU * (g + 1))
                    parts = [negmax_parts[:, g % 2, :, k, :] for k in range(PARTS)]
                    steps = Steps(dve, negmax_steps, 4)
                    steps.begin(G * b.n + g)
                    steps.did(dve.tensor_copy(parts[0], negmax[:, g % 2]))
                    steps.settle()
                    steps.did(dve.tensor_tensor(negmax_rest[:, :, :], negmax[:, g % 2], parts[0], ALU.subtract))
                    steps.settle()
                    steps.did(dve.tensor_copy(parts[1], negmax_rest[:, :, :]))
                    steps.settle()
                    steps.did(dve.tensor_tensor(parts[2], negmax_rest[:, :, :], parts[1], ALU.subtract))

            def take(cur, pos):
                _, step, arg = MISC[pos]
                if step in ("xt", "mt", "at", "ht"):
                    return
                nxt, last = cur.plus(1), cur.plus(-1)
                wait_misc(dve, cur, step, arg)
                if step in ("qa", "qb"):
                    k = int(step == "qb")
                    if k == 0 and (nxt.later_than(1) or arg == 2):
                        dve.wait_ge(split_steps, SPLITS * (3 * nxt.n + arg - 2) + 1)
                    n = P if arg < NC else G * DH
                    bias = bq[:, k, arg:arg + 1] if arg < NC else bk[:, k:k + 1]
                    dve.scalar_tensor_tensor(out=roped[0:n, (nxt.parity + arg) % 2, k, :], in0=ps_misc[0:n, :], scalar=bias,
                                             in1=rope[0:n, int(arg == NC), k, :], op0=ALU.add, op1=ALU.mult) \
                        .then_inc(misc_taken, 1)
                elif step == "v":
                    if nxt.later_than(2):
                        dve.wait_ge(weighed, UB * (nxt.n - 1))
                    dve.tensor_tensor(va[:, nxt.parity], ps_misc[:, :].rearrange("p (j n) -> p j n", j=NT),
                                      bv[:, :].unsqueeze(1).to_broadcast([P, NT, G * 2 * DH]), ALU.add) \
                        .then_inc(misc_taken, 1)
                elif step == "ot":
                    if arg == 0:
                        post.begin(last.n)
                    src = ps_misc[:, :].rearrange("p (h w) -> p h w", h=H)
                    post.did(dve.reciprocal(denom[:, :], src[:, :, DH]))
                    post.settle()
                    dve.tensor_tensor(heads[:, arg, :].rearrange("p (h w) -> p h w", h=H), src[:, :, 0:DH],
                                      denom[:, :].unsqueeze(2).to_broadcast([P, H, DH]), ALU.mult) \
                        .then_inc(misc_taken, 1)
                elif step == "op":
                    dve.tensor_tensor(proj[:, 2 * arg:2 * arg + 2, :],
                                      ps_misc[:, :].rearrange("p (j n) -> p j n", j=2),
                                      bo[:, :].unsqueeze(1).to_broadcast([P, 2, D]), ALU.add) \
                        .then_inc(misc_taken, 1)
                    if arg == 1:
                        dve.wait_ge(misc_taken, misc_number(cur, pos) + 1)
                        moments_of(post, proj)
                elif step == "rt":
                    dve.tensor_tensor(logits[:, :, :],
                                      ps_misc[:, 0:NT * E].rearrange("p (j e) -> p j e", j=NT),
                                      gate_b[:, :].unsqueeze(1).to_broadcast([P, NT, E]), ALU.add) \
                        .then_inc(misc_taken, 1)
                elif step == "cn":
                    count(cur, pos, last)

            def choose(last):
                dve.wait_ge(gates_exped, last.n + 1)
                post.did(dve.tensor_scalar(gates[:, :, :], gates[:, :, :], 1.0, None, ALU.add))
                post.settle()
                post.did(dve.reciprocal(gates[:, :, :], gates[:, :, :]))
                post.settle()
                pause()
                for j in range(NT):
                    post.did(dve.max(top[:, j, :], gates[:, j, :]))

            def weigh_choice(last):
                post.settle()
                pause()
                for j in range(NT):
                    post.did(dve.max_index(top_at[:, j, :], top[:, j, :], gates[:, j, :]))
                post.did(dve.tensor_tensor(top_sum[:, :], top[:, :, 0], top[:, :, 1], ALU.add))
                post.settle()
                post.did(dve.tensor_copy(expert[:, :, :], top_at[:, :, 0:2]))
                post.did(dve.reciprocal(top_sum[:, :], top_sum[:, :]))
                post.settle()
                post.did(dve.tensor_tensor(routed_w[:, last.n], top[:, :, 0:2],
                                           top_sum[:, :].unsqueeze(2).to_broadcast([P, NT, 2]), ALU.mult))
                post.did(dve.tensor_copy(routed_e[:, last.n], expert[:, :, :]))
                for k in range(2):
                    post.did(dve.tensor_tensor(onehot[:, :, k, :], iota_e[:, :].unsqueeze(1).to_broadcast([P, NT, E]),
                                               expert[:, :, k].unsqueeze(2).to_broadcast([P, NT, E]),
                                               ALU.is_equal))
                post.settle()
                dve.tensor_tensor(chosen[:, :, :], onehot[:, :, 0, :], onehot[:, :, 1, :], ALU.add) \
                    .then_inc(chosen_ready, 1)

            def count(cur, pos, last):
                post.did(dve.tensor_copy(counts[:, 0, :], counts[:, NT, :]))
                for j in range(NT):
                    post.settle()
                    post.did(dve.tensor_tensor(counts[:, j + 1, :], counts[:, j, :],
                                               ps_misc[:, (NT + j) * E:(NT + j + 1) * E], ALU.add))
                post.settle()
                dve.tensor_tensor(place[:, :, :], ps_misc[:, 0:NT * E].rearrange("p (j e) -> p j e", j=NT),
                                  counts[:, 0:NT, :], ALU.add).then_inc(misc_taken, 1)
                dve.wait_ge(misc_taken, misc_number(cur, pos) + 1)
                for k in range(2):
                    post.did(dve.tensor_tensor(placed[:, :, k, :], onehot[:, :, k, :], place[:, :, :], ALU.mult))
                post.settle()
                post.did(dve.tensor_reduce(routed_pos[:, last.n], placed[:, :, :, :], AX_X, ALU.add))
                post.settle()
                if last.later_than(2):
                    dve.wait_ge(scattered[last.parity], 16 * 2 * NT * last.half)
                post.did(dve.tensor_copy(token_i[last.parity][:, :], token[:, :]))
                post.did(dve.tensor_scalar(token[:, :], token[:, :], float(T), None, ALU.add))
                post.settle()
                dve.scalar_tensor_tensor(out=slot[last.parity][:, :, :], in0=expert[:, :, :], scalar=float(TOKENS),
                                         in1=routed_pos[:, last.n], op0=ALU.mult, op1=ALU.add) \
                    .then_inc(slots_ready, 1)
                post.end()

            def body(cur):
                nxt, last = cur.plus(1), cur.plus(-1)
                if cur.offset == -1:
                    first_moments(nxt)
                    first_normalise(nxt)
                for n in range(UB):
                    reduce_max(cur, n)
                    for pos, (at, step, arg) in enumerate(MISC):
                        if at == n and active(cur, step, arg):
                            take(cur, pos)
                    if last.exists:
                        if n == 13:
                            normalise(post, proj, proj, None)
                        if n == 14:
                            add_residual(last)
                        if n == 15:
                            second_normalise(last)
                        if n == 21:
                            choose(last)
                        if n == 22:
                            weigh_choice(last)
                    if nxt.plus(1).exists:
                        if n == 16:
                            first_moments(nxt.plus(1))
                        if n == 17:
                            first_normalise(nxt.plus(1))

            rounds(dve, body)


POST_STEPS = (NT
              + 2 * (NT + NT + RSQRT_STEPS) + NT
              + 2 + NT + NT + 1 + 2 + 1 + 1 + 2
              + 1 + NT + 2 + 1 + 2)
N_CONSTS = 16
N_LOADS = 13
N_ZEROS = -(-(LIST // 544) // P) + 1


def expert_phases(nc, a, out, v):
    ctx = ExitStack()
    with ctx:
        def sb(name, shape, dt=F32):
            return ctx.enter_context(nc.sbuf_tensor(name, shape, dt))

        def psum(name, shape):
            return ctx.enter_context(nc.psum_tensor(name, shape, F32))

        def sem(name):
            return ctx.enter_context(nc.semaphore(name))

        wgu, wd, ident, counts, iota_e = (v[n] for n in ("wgu", "wd", "ident", "counts", "iota_e"))
        routed_e, routed_pos, routed_w = (v[n] for n in ("routed_e", "routed_pos", "routed_w"))
        id_list, y_dram, h2_dram, x1_dram = (v[n] for n in ("id_list", "y_dram", "h2_dram", "x1_dram"))

        tile_ends = sb("tile_ends", [P, E])
        tiles_of = sb("tiles_of", [P, E])
        tiles_i = sb("tiles_i", [P, E], I32)
        jumps = sb("jumps", [P, E])
        tile_no = sb("tile_no", [1, TILES])
        past = sb("past", [1, TILES, E])
        tile_e = sb("tile_e", [1, TILES])
        tile_at = sb("tile_at", [1, TILES])
        tile_e_i = sb("tile_e_i", [1, TILES], I32)
        tile_at_i = sb("tile_at_i", [1, TILES], I32)
        first_row = sb("first_row", [P, E])
        y_row = sb("y_row", [P, B * NT * 2])
        y_hot = sb("y_hot", [P, B * NT * 2, E])
        y_row_i = sb("y_row_i", [P, B * NT * 2], U32)

        ids = [sb(f"ids{k}", [P, 1], I32) for k in range(8)]
        rows = sb("rows", [P, 8, D])
        rows_t = sb("rows_t", [P, 2, NC, P])
        gate = sb("gate", [P, 2, I])
        hid = sb("hid", [P, 2, I])
        hid_t = sb("hid_t", [P, 2, P])
        ysb = sb("ysb", [P, 2, D])
        y_in = sb("y_in", [P, 8, 2, D])
        y_row_t = [sb(f"y_row_t{k}", [P, 2], U32) for k in range(8)]
        summed = sb("summed", [P, 2, NT, D])
        x1_in = sb("x1_in", [P, NT, D])
        final = sb("final", [P, NT, D])
        stats = sb("stats2", [P, NT, 6])
        moments = sb("moments2", [P, NT, 2])
        rstd = sb("rstd2", [P, 2, NT])
        shift = sb("shift", [P, 2, NT])
        work = [sb(f"work2{k}", [P, NT]) for k in range(2)]

        ps_t = psum("ps_t", [P, 2, T])
        ps_gu = psum("ps_gu", [P, 2, T])
        ps_ht = psum("ps_ht", [P, 2, T])
        ps_y = psum("ps_y", [P, 2, T])

        plan_steps = sem("plan_steps")
        numbered = sem("numbered")
        plan_ready = sem("plan_ready")
        out_stored = sem("out_stored")

        plan_block = nc.Block()
        block = plan_block.__enter__()

        @block.gpsimd
        def _(pool):
            pool.iota(tile_no[:, :], pattern=[[1, TILES]], base=0, channel_multiplier=0,
                      allow_small_or_imprecise_dtypes=True).then_inc(numbered, 1)

        @block.vector
        def _(dve):
            plan = Steps(dve, plan_steps, 0)
            plan.begin(0)

            def do(ins):
                plan.did(ins)
                plan.settle()

            do(dve.tensor_scalar(tiles_i[:, :], counts[:, NT, :], float(P - 1), None, ALU.add))
            do(dve.tensor_scalar(tiles_i[:, :], tiles_i[:, :], 7, None, ALU.arith_shift_right))
            do(dve.tensor_copy(tiles_of[:, :], tiles_i[:, :]))
            do(dve.tensor_copy(tile_ends[:, 0:1], tiles_of[:, 0:1]))
            for e in range(1, E):
                do(dve.tensor_tensor(tile_ends[:, e:e + 1], tile_ends[:, e - 1:e], tiles_of[:, e:e + 1], ALU.add))
            dve.wait_ge(numbered, 1)
            do(dve.tensor_tensor(past[:, :, :], tile_no[:, :].unsqueeze(2).to_broadcast([1, TILES, E]),
                                 tile_ends[0:1, :].unsqueeze(1).to_broadcast([1, TILES, E]), ALU.is_ge))
            do(dve.tensor_reduce(tile_e[:, :], past[:, :, 0:E - 1], AX_X, ALU.add))
            do(dve.tensor_scalar(jumps[:, :], tiles_of[:, :], -float(P), float(TOKENS), ALU.mult, ALU.add))
            do(dve.tensor_tensor(past[:, :, :], past[:, :, :],
                                 jumps[0:1, :].unsqueeze(1).to_broadcast([1, TILES, E]), ALU.mult))
            do(dve.tensor_reduce(tile_at[:, :], past[:, :, 0:E - 1], AX_X, ALU.add))
            do(dve.scalar_tensor_tensor(out=tile_at[:, :], in0=tile_no[:, :], scalar=float(P), in1=tile_at[:, :],
                                        op0=ALU.mult, op1=ALU.add))
            do(dve.tensor_copy(tile_e_i[:, :], tile_e[:, :]))
            do(dve.tensor_copy(tile_at_i[:, :], tile_at[:, :]))
            do(dve.tensor_tensor(first_row[:, :], tile_ends[:, :], tiles_of[:, :], ALU.subtract))
            do(dve.tensor_scalar(first_row[:, :], first_row[:, :], float(P), None, ALU.mult))
            n = B * NT * 2
            flat = "p b j k -> p (b j k)"
            do(dve.tensor_tensor(y_hot[:, :, :], iota_e[:, :].unsqueeze(1).to_broadcast([P, n, E]),
                                 routed_e[:, :, :, :].rearrange(flat).unsqueeze(2).to_broadcast([P, n, E]),
                                 ALU.is_equal))
            do(dve.tensor_tensor(y_hot[:, :, :], y_hot[:, :, :],
                                 first_row[:, :].unsqueeze(1).to_broadcast([P, n, E]), ALU.mult))
            do(dve.tensor_reduce(y_row[:, :], y_hot[:, :, :], AX_X, ALU.add))
            do(dve.tensor_tensor(y_row[:, :], y_row[:, :], routed_pos[:, :, :, :].rearrange(flat), ALU.add))
            do(dve.tensor_copy(y_row_i[:, :], y_row[:, :]))

        plan_block.__exit__(None, None, None)
        for shared in (False, True):
            mlp_phase(nc, a, out, v, locals(), shared)


def mlp_phase(nc, a, out, v, w, shared):
    wgu, wd, ident = (v[n] for n in ("wgu", "wd", "ident"))
    routed_w, id_list, y_dram, h2_dram, x1_dram = (
        v[n] for n in ("routed_w", "id_list", "y_dram", "h2_dram", "x1_dram"))
    (shift, ids, rows, rows_t, gate, hid, hid_t, ysb, y_in, y_row_t, summed, x1_in, final, stats, moments, rstd, work) = (
        w[n] for n in ("shift", "ids", "rows", "rows_t", "gate", "hid", "hid_t", "ysb", "y_in", "y_row_t", "summed",
                       "x1_in", "final", "stats", "moments", "rstd", "work"))
    (ps_t, ps_gu, ps_ht, ps_y, tile_e_i, tile_at_i, y_row_i, out_stored) = (
        w[n] for n in ("ps_t", "ps_gu", "ps_ht", "ps_y", "tile_e_i", "tile_at_i", "y_row_i", "out_stored"))
    tiles = B * NT if shared else TILES
    unroll = 8
    tag = "s" if shared else "r"
    DEPTH = 8
    AHEAD = 5
    LAG = 5 if shared else 3

    ctx = ExitStack()
    with ctx:
        def sem(name):
            return ctx.enter_context(nc.semaphore(f"{name}_{tag}"))

        ids_loaded = [sem(f"ids_loaded{k}") for k in range(DEPTH)]
        rows_loaded = [sem(f"rows_loaded{k}") for k in range(DEPTH)]
        turned, turned_out = sem("turned"), sem("turned_out")
        hidden, gated, hid_ready = sem("hidden"), sem("gated"), sem("hid_ready")
        hid_turned, hid_t_ready = sem("hid_turned"), sem("hid_t_ready")
        y_done, y_taken = sem("y_done"), sem("y_taken")
        y_stored = [sem(f"y_stored{k}") for k in range(2)]
        pair_added = sem("pair_added")
        paused = sem("paused")
        y_row_ready = sem("y_row_ready")
        y_loaded = [sem(f"y_loaded{k}") for k in range(DEPTH)]
        x1_loaded = sem("x1_loaded")
        norm_steps, norm_ready, normed, norm_done = (
            sem("norm_steps"), sem("norm_ready"), sem("normed"), sem("norm_done"))

        class Tile:

            def __init__(self, offset, turn=None):
                self.offset, self.turn = offset, turn
                self.n = offset if turn is None else unroll * turn + offset

            def plus(self, k):
                return Tile(self.offset + k, self.turn)

            @property
            def exists(self):
                return self.turn is not None or 0 <= self.offset < tiles

            def later_than(self, k):
                return self.turn is not None or self.offset >= k

            def buf(self, n):
                return self.offset % n

            def round(self, n):
                return self.offset // n if self.turn is None else (unroll // n) * self.turn + self.offset // n

        def steps_of(eng, body, first=-1, last=2):
            lead = 8
            turns = (tiles - 2 * lead) // unroll
            for k in range(first, lead):
                body(Tile(k))
            with eng.Fori(0, turns) as turn:
                for u in range(unroll):
                    body(Tile(lead + u, turn))
            for k in range(lead + unroll * turns, tiles + last):
                body(Tile(k))

        block = ctx.enter_context(nc.Block())

        @block.sync
        def _(sp):
            if not shared:
                sp.wait_ge(v["h2_stored"], 16 * B)
                sp.wait_ge(v["x1_stored"], 16 * B)
                for k in range(2):
                    sp.wait_ge(v["scattered"][k], 16 * NT * B)

            def load(t):
                k = t.buf(DEPTH)
                if not shared:
                    at = sp.value_load(tile_at_i[0:1, bass.ds(t.n, 1)], min_val=0, max_val=LIST - P)
                    sp.dma_start(ids[k][:, :], id_list[bass.ds(at, P), :]).then_inc(ids_loaded[k], 16)
                else:
                    if t.later_than(DEPTH):
                        sp.wait_ge(y_done, t.n - DEPTH + 1)
                    sp.dma_start(rows[:, k, :], h2_dram.rearrange("b (j p) d -> (b j) p d", p=P)[t.n]) \
                        .then_inc(rows_loaded[k], 16)

            def store(t):
                if not shared:
                    k = t.buf(2)
                    sp.wait_ge(y_taken, t.n + 1)
                    sp.dma_start(y_dram.rearrange("(n p) d -> n p d", p=P)[t.n], ysb[:, k, :]) \
                        .then_inc(y_stored[k], 16)
                elif t.offset % NT == NT - 1:
                    b = t.round(NT)
                    sp.wait_ge(norm_done, b + 1)
                    sp.dma_start(out[b].rearrange("(j p) d -> p j d", p=P), final[:, :, :]) \
                        .then_inc(out_stored, 16)

            def body(t):
                if t.plus(-LAG).exists:
                    store(t.plus(-LAG))
                if t.plus(AHEAD).exists:
                    load(t.plus(AHEAD))
                if shared and t.exists and t.offset % NT == 2:
                    b = t.round(NT)
                    if t.later_than(NT):
                        sp.wait_ge(norm_done, b)
                    sp.dma_start(x1_in[:, :, :], x1_dram[b].rearrange("(j p) d -> p j d", p=P)) \
                        .then_inc(x1_loaded, 16)

            steps_of(sp, body, first=-AHEAD, last=LAG)
            if shared:
                sp.wait_ge(out_stored, 16 * B)
            else:
                for k in range(2):
                    sp.wait_ge(y_stored[k], 16 * TILES // 2)

        @block.gpsimd
        def _(pool):
            pause = Pause(pool, v["pool_cell"], v["zero_col"][0:1, 0:1], paused)

            def body(t):
                k = t.buf(DEPTH)
                if not t.exists:
                    return
                if not shared:
                    pool.wait_ge(ids_loaded[k], 16 * (t.round(DEPTH) + 1))
                    if t.later_than(DEPTH):
                        pool.wait_ge(turned, t.n - DEPTH + 1)
                    pause(t.n, t.later_than(1))
                    pool.indirect_dma_start(
                        out=rows[:, k, :], out_offset=None, in_=h2_dram.rearrange("b t d -> (b t) d"),
                        in_offset=bass.IndirectOffsetOnAxis(ap=ids[k][:, 0:1].bitcast(U32), axis=0),
                    ).then_inc(rows_loaded[k], 16)
                else:
                    k2 = t.buf(DEPTH)
                    pool.wait_ge(y_row_ready, t.n + 1)
                    if t.later_than(DEPTH):
                        pool.wait_ge(pair_added, t.n - DEPTH + 1)
                    pause(t.n, t.later_than(1))
                    for c in range(2):
                        pool.indirect_dma_start(
                            out=y_in[:, k2, c, :], out_offset=None, in_=y_dram[:, :],
                            in_offset=bass.IndirectOffsetOnAxis(ap=y_row_t[k][:, c:c + 1], axis=0),
                        ).then_inc(y_loaded[k2], 16)

            steps_of(pool, body)

        @block.tensor
        def _(pe):
            pe.wait_ge(v["experts_in"], 16 * 3 * (E + 1))

            known = {}

            def expert(t):
                if shared:
                    return E
                if (t.turn is None, t.offset) not in known:
                    known[t.turn is None, t.offset] = pe.value_load(tile_e_i[0:1, bass.ds(t.n, 1)],
                                                                    min_val=0, max_val=E - 1)
                return known[t.turn is None, t.offset]

            def turn_rows(t):
                pe.wait_ge(rows_loaded[t.buf(DEPTH)], 16 * (t.round(DEPTH) + 1))
                if t.later_than(2):
                    pe.wait_ge(turned_out, t.n - 1)
                for c in range(NC):
                    ins = pe.transpose(ps_t[:, t.buf(2), c * P:(c + 1) * P],
                                       rows[:, t.buf(DEPTH), c * P:(c + 1) * P], ident[:, :])
                ins.then_inc(turned, 1)

            def gate_up(t, e):
                pe.wait_ge(turned_out, t.n + 1)
                if t.later_than(2):
                    pe.wait_ge(hid_ready, t.n - 1)
                for c in range(NC):
                    ins = pe.matmul(ps_gu[:, t.buf(2), 0:2 * I], rows_t[:, t.buf(2), c, :], wgu[:, e, c, :],
                                    start=(c == 0), stop=(c == NC - 1))
                ins.then_inc(hidden, 1)

            def turn_hidden(t):
                pe.wait_ge(hid_ready, t.n + 1)
                if t.later_than(2):
                    pe.wait_ge(hid_t_ready, t.n - 1)
                pe.transpose(ps_ht[:, t.buf(2), 0:P], hid[:, t.buf(2), :], ident[:, :]).then_inc(hid_turned, 1)

            def down(t, e):
                pe.wait_ge(hid_t_ready, t.n + 1)
                if t.later_than(2):
                    pe.wait_ge(y_taken, t.n - 1)
                ins = pe.matmul(ps_y[:, t.buf(2), 0:D], hid_t[:, t.buf(2), :], wd[:, e, :],
                                start=True, stop=not shared)
                if shared:
                    ins = pe.matmul(ps_y[:, t.buf(2), 0:D], ident[:, :], rows[:, t.buf(DEPTH), :],
                                    start=False, stop=True)
                ins.then_inc(y_done, 1)

            def body(t):
                e_up = expert(t) if t.exists else None
                e_down = expert(t.plus(-2)) if t.plus(-2).exists else None
                if t.plus(-2).exists:
                    turn_hidden(t.plus(-2))
                if t.plus(1).exists:
                    turn_rows(t.plus(1))
                if t.exists:
                    gate_up(t, e_up)
                if t.plus(-2).exists:
                    down(t.plus(-2), e_down)

            steps_of(pe, body)

        @block.scalar
        def _(act):
            def body(t):
                if t.plus(-2).exists:
                    h = t.plus(-2)
                    act.wait_ge(hid_turned, h.n + 1)
                    if h.later_than(2):
                        act.wait_ge(y_done, h.n - 1)
                    act.copy(hid_t[:, h.buf(2), :], ps_ht[:, h.buf(2), 0:P]).then_inc(hid_t_ready, 1)
                if t.plus(1).exists:
                    r = t.plus(1)
                    act.wait_ge(turned, r.n + 1)
                    if r.later_than(2):
                        act.wait_ge(hidden, r.n - 1)
                    act.copy(rows_t[:, r.buf(2)].rearrange("p c n -> p (c n)"), ps_t[:, r.buf(2), 0:D]) \
                        .then_inc(turned_out, 1)
                if t.exists:
                    act.wait_ge(hidden, t.n + 1)
                    if t.later_than(2):
                        act.wait_ge(hid_ready, t.n - 1)
                    act.activation(gate[:, t.buf(2), :], ps_gu[:, t.buf(2), 0:I], ACT.Silu).then_inc(gated, 1)
                if shared and t.plus(-3).exists and t.plus(-3).offset % NT == NT - 1:
                    last = t.plus(-3)
                    b, k = last.round(NT), last.offset // NT % 2
                    act.wait_ge(norm_ready, b + 1)
                    if last.later_than(NT):
                        act.wait_ge(out_stored, 16 * b)
                    for i in range(NT):
                        ins = act.activation(final[:, i, :], summed[:, k, i, :], ACT.Identity,
                                             bias=shift[:, k, i:i + 1], scale=rstd[:, k, i:i + 1])
                    ins.then_inc(normed, 1)

            steps_of(act, body, last=3)

        @block.vector
        def _(dve):
            pause = Pause(dve, v["dve_cell"])

            norm = Steps(dve, norm_steps, NT + NT + RSQRT_STEPS)

            def multiply(t):
                k = t.buf(2)
                dve.wait_ge(gated, t.n + 1)
                if t.later_than(2):
                    dve.wait_ge(hid_turned, t.n - 1)
                dve.tensor_tensor(hid[:, k, :], ps_gu[:, k, I:2 * I], gate[:, k, :], ALU.mult) \
                    .then_inc(hid_ready, 1)

            def take_y(t):
                dve.wait_ge(y_done, t.n + 1)
                if t.later_than(2):
                    dve.wait_ge(y_stored[t.buf(2)], 16 * t.round(2))
                dve.tensor_copy(ysb[:, t.buf(2), :], ps_y[:, t.buf(2), 0:D]).then_inc(y_taken, 1)

            def name_rows(t):
                k = t.buf(DEPTH)
                if t.later_than(DEPTH):
                    dve.wait_ge(y_loaded[k], 32 * t.round(DEPTH))
                dve.tensor_copy(y_row_t[k][:, :], y_row_i[:, bass.ds(2 * t.n, 2)]).then_inc(y_row_ready, 1)

            def combine(t):
                j, k2, k8 = t.offset % NT, t.buf(2), t.buf(DEPTH)
                b, k = t.round(NT), t.offset // NT % 2
                norm.begin(b)
                norm.c = j
                wt = routed_w[:, b, j, :]
                s = summed[:, k, j, :]
                dve.wait_ge(y_done, t.n + 1)
                dve.wait_ge(y_loaded[k8], 32 * (t.round(DEPTH) + 1))
                dve.scalar_tensor_tensor(out=s, in0=y_in[:, k8, 0, :], scalar=wt[:, 0:1], in1=ps_y[:, k2, 0:D],
                                         op0=ALU.mult, op1=ALU.add).then_inc(y_taken, 1)
                dve.wait_ge(y_taken, t.n + 1)
                dve.scalar_tensor_tensor(out=s, in0=y_in[:, k8, 1, :], scalar=wt[:, 1:2], in1=s,
                                         op0=ALU.mult, op1=ALU.add).then_inc(pair_added, 1)
                dve.wait_ge(pair_added, t.n + 1)
                norm.did(dve.bn_stats(stats[:, j, :], s))
                if j == NT - 1:
                    norm.settle()
                    pause()
                    for i in range(NT):
                        norm.did(dve.bn_aggr(moments[:, i, :], stats[:, i, :]))
                    norm.settle()
                    rsqrt(dve, norm, rstd[:, k, :], moments[:, :, 1], [x[:, :] for x in work])
                    norm.end()
                    dve.scalar_tensor_tensor(out=shift[:, k, :], in0=moments[:, :, 0], scalar=-1.0,
                                             in1=rstd[:, k, :], op0=ALU.mult, op1=ALU.mult) \
                        .then_inc(norm_ready, 1)

            def finish(t):
                b = t.round(NT)
                dve.wait_ge(normed, b + 1)
                dve.wait_ge(x1_loaded, 16 * (b + 1))
                dve.tensor_tensor(final[:, :, :], final[:, :, :], x1_in[:, :, :], ALU.add).then_inc(norm_done, 1)

            def body(t):
                if shared and t.plus(AHEAD).exists:
                    name_rows(t.plus(AHEAD))
                if t.exists:
                    multiply(t)
                if t.plus(-2).exists:
                    (combine if shared else take_y)(t.plus(-2))
                if shared and t.plus(-4).exists and t.plus(-4).offset % NT == NT - 1:
                    finish(t.plus(-4))

            steps_of(dve, body, first=-AHEAD, last=4)


def kernel(**inputs):
    import concourse.bacc as bacc
    from concourse.bass_utils import run_bass_kernel_spmd as run

    x = {k: np.ascontiguousarray(np.asarray(w)) for k, w in inputs.items()}
    f = lambda n: x["L0_" + n]
    swap_q, swap_k = np.arange(D) ^ 1, np.arange(G * DH) ^ 1
    freq = np.exp(-(np.arange(0, DH, 2, dtype=np.float32) / np.float32(DH)) * np.log(np.float32(10000.0)))
    angle = np.arange(T, dtype=np.float32)[:, None] * freq.astype(np.float32)
    row = np.arange(P) % DH
    cos = np.cos(angle).astype(np.float32).T[row // 2]
    sin = np.sin(angle).astype(np.float32).T[row // 2] * np.where(row % 2, 1, -1).astype(np.float32)[:, None]
    scale = np.float32(1 / np.sqrt(DH))
    rope = np.stack([np.stack([cos * scale, sin * scale], 1), np.stack([cos, sin], 1)], 1).astype(np.float32)
    wv = np.zeros((D, G, 2, DH), np.float32)
    wv[:, :, 0] = f("attn_Wv").reshape(D, G, DH)
    bv = np.ones((G, 2, DH), np.float32)
    bv[:, 0] = f("attn_bv").reshape(G, DH)
    arrays = {
        "x": f("attn_x"), "wq0": f("attn_Wq"), "wq1": f("attn_Wq")[:, swap_q], "wk0": f("attn_Wk"),
        "wk1": f("attn_Wk")[:, swap_k],
        "bq": np.stack([f("attn_bq").reshape(NC, P).T, f("attn_bq")[swap_q].reshape(NC, P).T], 1),
        "bk": np.stack([f("attn_bk"), f("attn_bk")[swap_k]], 1),
        "rope": rope, "wv": wv.reshape(D, -1), "bv": bv.reshape(-1), "wo": f("attn_Wo"), "bo": f("attn_bo"),
        "gate_w": f("ffn_gate_w"), "gate_b": f("ffn_gate_b"), "eg": f("ffn_experts_wg"), "eu": f("ffn_experts_wu"),
        "ed": f("ffn_experts_wd"), "sg": f("ffn_shared_wg"), "su": f("ffn_shared_wu"), "sd": f("ffn_shared_wd"),
    }
    nc = bacc.Bacc("TRN2", target_bir_lowering=False, num_devices=1)
    ins = {}
    for k in arrays:
        arrays[k] = np.ascontiguousarray(arrays[k])
        ins[k] = nc.dram_tensor(f"in_{k}", arrays[k].shape, F32, kind="ExternalInput").ap()
    out = nc.dram_tensor("out_0", (B, T, D), F32, kind="ExternalOutput").ap()
    layer(nc, ins, out)
    r = run(nc, [{f"in_{k}": w for k, w in arrays.items()}], core_ids=[0])
    return r.results[0]["out_0"]
```
